# Optimizing a Trainium2 kernel written in Bass

```python
import numpy as np
import jax
import jax.numpy as jnp

def _softmax(x, axis=-1):
    return jax.nn.softmax(x, axis=axis)

def _gelu(x):
    return jax.nn.gelu(x, approximate=True)

def _silu(x):
    return jax.nn.silu(x)

def _sigmoid(x):
    return jax.nn.sigmoid(x)

def _layernorm(x, axis=-1, eps=1e-05):
    m = jnp.mean(x, axis=axis, keepdims=True)
    v = jnp.var(x, axis=axis, keepdims=True)
    return (x - m) / jnp.sqrt(v + eps)

def _scatter_add(tgt, idx, src, axis=0):
    return tgt.at[idx].add(src)

def _segment_sum(src, seg, n):
    return jax.ops.segment_sum(src, seg, n)
kernel_name = 'mk_xattn_ffn_d1_seqx_r4_bff9a6'

def setup_inputs(seed: int=0):
    np.random.seed(seed)
    _w = jnp.asarray

    def _rec_inputs():
        import jax
        import jax.numpy as jnp
        _rk = jax.random.key(seed)
        x = -0.0002928 + 1 * jax.random.normal(jax.random.fold_in(_rk, 1), (8, 112, 256), jnp.float32)
        _lenS = 112 - jax.random.randint(jax.random.fold_in(_rk, 7), (8,), 0, max(1, 112 // 4) + 1, jnp.int32)
        _lenS2 = 375 - jax.random.randint(jax.random.fold_in(_rk, 8), (8,), 0, max(1, 375 // 4) + 1, jnp.int32)
        _ctx_1024P = jax.random.normal(jax.random.fold_in(_rk, 11), (8, 16, 256), jnp.float32)
        _ctx_1024c = jax.random.dirichlet(jax.random.fold_in(_rk, 511), 0.3 * jnp.ones((16,), jnp.float32), (8, 375))
        _ctx_1024t = jnp.einsum('bsk,bkd->bsd', _ctx_1024c, _ctx_1024P)
        _ctx_1024t = _ctx_1024t * jax.lax.rsqrt(jnp.mean(jnp.square(_ctx_1024t)) + 1e-12) * 0.953939
        ctx_1024 = -1.39393e-06 + 0.999914 * (_ctx_1024t + 0.3 * jax.random.normal(jax.random.fold_in(_rk, 611), (8, 375, 256), jnp.float32))
        _validS = jnp.arange(112)[None, :] < _lenS[:, None]
        _validS2 = jnp.arange(375)[None, :] < _lenS2[:, None]
        _causal = jnp.tril(jnp.ones((112, 112), dtype=bool))
        mask_Bx1xSxS2_ff0 = jnp.where(jnp.ones((8, 1, 112, 375), dtype=bool), 0.0, -1000000000.0).astype(jnp.float32)
        return (x, ctx_1024, mask_Bx1xSxS2_ff0)
    x, ctx_1024, mask_Bx1xSxS2_ff0 = _rec_inputs()

    def _L0_xattn_setup():
        import jax, jax.numpy as jnp
        import numpy as np
        HIDDEN = 256
        HEADS = 16
        N, T1, T2 = (2, 512, 512)

        def _split_heads(x):
            n, t, e = x.shape
            return x.reshape(n, t, HEADS, e // HEADS).transpose(0, 2, 1, 3)
        key = jax.random.key(seed)
        k1, k2, k3, k4 = jax.random.split(key, 4)
        q = jax.random.normal(k1, (N, T1, HIDDEN), dtype=jnp.float32)
        encoder_k = jax.random.normal(k2, (N, T2, HIDDEN), dtype=jnp.float32)
        encoder_v = jax.random.normal(k3, (N, T2, HIDDEN), dtype=jnp.float32)
        encoder_attention_mask = jnp.zeros((N, 1, T2, T2), dtype=jnp.float32)
        wo_w = jax.random.normal(k4, (HIDDEN, HIDDEN), dtype=jnp.float32) * (1.0 / np.sqrt(HIDDEN))
        wo_b = jnp.zeros((HIDDEN,), dtype=jnp.float32)
        return {'q': q, 'encoder_k': encoder_k, 'encoder_v': encoder_v, 'encoder_attention_mask': encoder_attention_mask, 'wo_w': wo_w, 'wo_b': wo_b}
    _L0_xattn_all = _L0_xattn_setup()
    _L0_xattn_in = {k: v for k, v in _L0_xattn_all.items() if k in ('wo_w', 'wo_b')}
    del _L0_xattn_all

    def _L0_ffn_setup():
        import jax, jax.numpy as jnp
        import numpy as np
        DIM = 256
        INTER = 128
        E = 32
        TOPK = 4
        GROUPS = 8
        TOPK_GROUPS = 4
        SHARED_INTER = 2 * INTER
        ROUTE_SCALE = 1.0
        B, S = (8, 1024)

        def _gate(xf, gw, gb):
            T = xf.shape[0]
            scores = jax.nn.softmax((xf @ gw + gb).astype(jnp.float32), axis=-1)
            original_scores = scores
            scores_g = scores.reshape(T, GROUPS, E // GROUPS)
            group_scores = jnp.sum(jax.lax.top_k(scores_g, 2)[0], axis=-1)
            gidx = jax.lax.top_k(group_scores, TOPK_GROUPS)[1]
            keep = jnp.zeros((T, GROUPS), bool).at[jnp.arange(T)[:, None], gidx].set(True)
            masked = jnp.where(keep[:, :, None], scores_g, -jnp.inf).reshape(T, E)
            indices = jax.lax.top_k(masked, TOPK)[1]
            weights = jnp.take_along_axis(original_scores, indices, axis=1) * ROUTE_SCALE
            return (weights.astype(xf.dtype), indices)
        key = jax.random.key(seed)
        ks = jax.random.split(key, 16)

        def xav(k, shape):
            fan_in, fan_out = (shape[-2], shape[-1])
            lim = np.sqrt(6.0 / (fan_in + fan_out))
            return jax.random.uniform(k, shape, jnp.float32, -lim, lim)
        return {'x': jax.random.normal(ks[0], (B, S, DIM), jnp.float32), 'gw': xav(ks[1], (DIM, E)), 'gb': jnp.zeros((E,), jnp.float32), 'w1': xav(ks[2], (E, DIM, INTER)), 'b1': jnp.zeros((E, INTER), jnp.float32), 'w3': xav(ks[3], (E, DIM, INTER)), 'b3': jnp.zeros((E, INTER), jnp.float32), 'w2': xav(ks[4], (E, INTER, DIM)), 'b2': jnp.zeros((E, DIM), jnp.float32), 'sw1': xav(ks[5], (DIM, SHARED_INTER)), 'sb1': jnp.zeros((SHARED_INTER,), jnp.float32), 'sw3': xav(ks[6], (DIM, SHARED_INTER)), 'sb3': jnp.zeros((SHARED_INTER,), jnp.float32), 'sw2': xav(ks[7], (SHARED_INTER, DIM)), 'sb2': jnp.zeros((DIM,), jnp.float32)}
    _L0_ffn_all = _L0_ffn_setup()
    _L0_ffn_in = {k: v for k, v in _L0_ffn_all.items() if k in ('gw', 'gb', 'w1', 'b1', 'w3', 'b3', 'w2', 'b2', 'sw1', 'sb1', 'sw3', 'sb3', 'sw2', 'sb2')}
    del _L0_ffn_all
    return {'x': x, 'ctx_1024': ctx_1024, 'mask_Bx1xSxS2_ff0': mask_Bx1xSxS2_ff0, 'L0_xattn_wo_w': _L0_xattn_in['wo_w'], 'L0_xattn_wo_b': _L0_xattn_in['wo_b'], 'L0_ffn_gw': _L0_ffn_in['gw'], 'L0_ffn_gb': _L0_ffn_in['gb'], 'L0_ffn_w1': _L0_ffn_in['w1'], 'L0_ffn_b1': _L0_ffn_in['b1'], 'L0_ffn_w3': _L0_ffn_in['w3'], 'L0_ffn_b3': _L0_ffn_in['b3'], 'L0_ffn_w2': _L0_ffn_in['w2'], 'L0_ffn_b2': _L0_ffn_in['b2'], 'L0_ffn_sw1': _L0_ffn_in['sw1'], 'L0_ffn_sb1': _L0_ffn_in['sb1'], 'L0_ffn_sw3': _L0_ffn_in['sw3'], 'L0_ffn_sb3': _L0_ffn_in['sb3'], 'L0_ffn_sw2': _L0_ffn_in['sw2'], 'L0_ffn_sb2': _L0_ffn_in['sb2']}

def reference(x, ctx_1024, mask_Bx1xSxS2_ff0, L0_xattn_wo_w, L0_xattn_wo_b, L0_ffn_gw, L0_ffn_gb, L0_ffn_w1, L0_ffn_b1, L0_ffn_w3, L0_ffn_b3, L0_ffn_w2, L0_ffn_b2, L0_ffn_sw1, L0_ffn_sb1, L0_ffn_sw3, L0_ffn_sb3, L0_ffn_sw2, L0_ffn_sb2):
    import jax
    import jax.numpy as jnp

    def _L0_xattn_ref(q, encoder_k, encoder_v, encoder_attention_mask, wo_w, wo_b):
        import jax, jax.numpy as jnp
        import numpy as np
        HIDDEN = 256
        HEADS = 16
        N, T1, T2 = (2, 512, 512)

        def _split_heads(x):
            n, t, e = x.shape
            return x.reshape(n, t, HEADS, e // HEADS).transpose(0, 2, 1, 3)
        qh = _split_heads(q)
        kh = _split_heads(encoder_k)
        vh = _split_heads(encoder_v)
        scores = jnp.einsum('bhqd,bhkd->bhqk', qh, kh) + encoder_attention_mask
        weights = jax.nn.softmax(scores, axis=-1)
        ctx = jnp.einsum('bhqk,bhkd->bhqd', weights, vh)
        ctx = ctx.transpose(0, 2, 1, 3).reshape(q.shape[0], q.shape[1], -1)
        return jax.nn.relu(ctx @ wo_w.T + wo_b)

    def _L0_ffn_ref(x, gw, gb, w1, b1, w3, b3, w2, b2, sw1, sb1, sw3, sb3, sw2, sb2):
        import jax, jax.numpy as jnp
        import numpy as np
        DIM = 256
        INTER = 128
        E = 32
        TOPK = 4
        GROUPS = 8
        TOPK_GROUPS = 4
        SHARED_INTER = 2 * INTER
        ROUTE_SCALE = 1.0
        B, S = (8, 1024)

        def _gate(xf, gw, gb):
            T = xf.shape[0]
            scores = jax.nn.softmax((xf @ gw + gb).astype(jnp.float32), axis=-1)
            original_scores = scores
            scores_g = scores.reshape(T, GROUPS, E // GROUPS)
            group_scores = jnp.sum(jax.lax.top_k(scores_g, 2)[0], axis=-1)
            gidx = jax.lax.top_k(group_scores, TOPK_GROUPS)[1]
            keep = jnp.zeros((T, GROUPS), bool).at[jnp.arange(T)[:, None], gidx].set(True)
            masked = jnp.where(keep[:, :, None], scores_g, -jnp.inf).reshape(T, E)
            indices = jax.lax.top_k(masked, TOPK)[1]
            weights = jnp.take_along_axis(original_scores, indices, axis=1) * ROUTE_SCALE
            return (weights.astype(xf.dtype), indices)
        shape = x.shape
        xf = x.reshape(-1, DIM)
        T = xf.shape[0]
        weights, indices = _gate(xf, gw, gb)
        cw = jnp.zeros((T, E), xf.dtype).at[jnp.arange(T)[:, None], indices].add(weights)

        def body(y, p):
            w1e, b1e, w3e, b3e, w2e, b2e, we = p
            h = jax.nn.silu(xf @ w1e + b1e) * (xf @ w3e + b3e)
            return (y + we[:, None] * (h @ w2e + b2e), None)
        y0 = jnp.zeros_like(xf)
        y, _ = jax.lax.scan(body, y0, (w1, b1, w3, b3, w2, b2, cw.T))
        z = jax.nn.silu(xf @ sw1 + sb1) * (xf @ sw3 + sb3) @ sw2 + sb2
        return (y + z).reshape(shape)
    x = x + _L0_xattn_ref(_layernorm(x, axis=-1), ctx_1024, ctx_1024, mask_Bx1xSxS2_ff0, L0_xattn_wo_w, L0_xattn_wo_b)
    x = x + _L0_ffn_ref(_layernorm(x, axis=-1), L0_ffn_gw, L0_ffn_gb, L0_ffn_w1, L0_ffn_b1, L0_ffn_w3, L0_ffn_b3, L0_ffn_w2, L0_ffn_b2, L0_ffn_sw1, L0_ffn_sb1, L0_ffn_sw3, L0_ffn_sb3, L0_ffn_sw2, L0_ffn_sb2)
    return x

_drawn_inputs = setup_inputs


def setup_inputs(seed=0):
    import zlib

    import numpy as np

    out = dict(_drawn_inputs(seed))
    spreads = {'L0_xattn_wo_b': (0.0, 0.1),
     'L0_ffn_gb': (0.0, 0.328),
     'L0_ffn_b1': (0.0, 0.587),
     'L0_ffn_b3': (0.0, 0.608),
     'L0_ffn_b2': (0.0, 0.354),
     'L0_ffn_sb1': (0.0, 0.1),
     'L0_ffn_sb3': (0.0, 0.1),
     'L0_ffn_sb2': (0.0, 0.1)}
    factors = {}
    for name, (base, spread) in spreads.items():
        noise = np.random.default_rng([zlib.crc32(name.encode()), seed]).standard_normal(out[name].shape)
        drawn = base * np.exp(spread * noise) if base else spread * noise
        out[name] = jnp.asarray(drawn.astype(out[name].dtype))
    for name, factor in factors.items():
        out[name] = (out[name] * factor).astype(out[name].dtype)
    return out
```

```python
from contextlib import ExitStack

import concourse.bass as bass
from concourse import mybir

ALU = mybir.AluOpType
ACT = mybir.ActivationFunctionType
AX = mybir.AxisListType
F32 = mybir.dt.float32
F32R = mybir.dt.float32r

P = 128
BANK = 512
HEADS = 16
TOPK = 4
KEEP_GROUPS = 4
GROUPS = 8
EPS = 1e-5
BIG = 3.0e38


def xattn_moe_kernel(nc, x, ctx, mask, wo_w, wo_b, gw, gb, w1, b1, w3, b3, w2, b2,
                     sw1, sb1, sw3, sb3, sw2, sb2, out):
    B, S, D = x.shape
    SK = ctx.shape[1]
    SKE = SK + SK % 2
    KT = 3
    KP = SK // KT
    DH = D // HEADS
    DK = D // P
    E, _, INTER = w1.shape
    NSH = sw1.shape[1] // INTER
    NE = E + NSH
    GE = E // GROUPS
    T = B * S
    NCH = 2
    CB = B // NCH
    CT = CB * S
    assert KP * KT == SK and INTER == P and DK == 2 and DH == 16 and NSH == 2 and CT <= BANK and B % 2 == 0

    NCP = HEADS
    CPB = NCP // 2
    NKU = HEADS // 2
    NQU = 2
    NPREP = NKU + NQU

    def aux_plan(last):
        plan = []
        for half in range(2):
            if half == 1 and last:
                spots = []
            else:
                spots = [0, 0, 1, 1, 2, 3, 4, 5, 6, 6]
            for n, at in enumerate(spots):
                plan.append((half * CPB + at, "prep", n, half, "DVE" if n % 2 else "ACT"))
        plan.append((CPB + 2, "ctxT", 0, 0, "ACT"))
        plan.append((CPB + 3, "proj", 0, 0, "DVE"))
        plan.append((NCP + 2, "ctxT", 0, 1, "ACT"))
        plan.append((NCP + 3, "proj", 0, 1, "DVE"))
        plan.sort(key=lambda u: u[0])
        return plan

    NAUX = len(aux_plan(False))

    def copied_by_dve(c):
        return c % 4 != 3

    def counts(upto):
        d = sum(copied_by_dve(c) for c in range(max(0, upto)))
        return d, max(0, upto) - d

    D_PAIR, A_PAIR = counts(NCP)

    scratch = nc.dram_tensor("gate_rows", (NE, T), F32, kind="Internal").ap()

    with ExitStack() as st:
        def sb(name, shape, dt=F32):
            return st.enter_context(nc.sbuf_tensor(name, shape, dt))

        def sem(name):
            return st.enter_context(nc.semaphore(name))

        ps = st.enter_context(nc.psum_tensor("ps", [P, 8, BANK], F32))

        ident = sb("ident", [P, P])
        x_sb = sb("x_sb", [S, B, D])
        q_sb = sb("q_sb", [S, B, D])
        x2 = sb("x2", [S, B, D])
        wo_raw = sb("wo_raw", [P, DK, D])
        woT = sb("woT", [P, DK, D])
        wob = sb("wob", [S, D])
        gw_sb = sb("gw_sb", [P, DK, E])
        gb_sb = sb("gb_sb", [S, E])
        b1r = sb("b1r", [NE, P])
        b3r = sb("b3r", [NE, P])
        b1T = sb("b1T", [P, NE])
        b3T = sb("b3T", [P, NE])
        b2a = sb("b2a", [NE, D])
        stats = sb("stats", [S, B, 6])
        mv = sb("mv", [S, B, 2])
        veps = sb("veps", [S, B])
        std = sb("std", [S, B])
        rstd = sb("rstd", [S, B])
        wr = sb("wr", [P, 2, 3, D])
        x_in = sem("x_in")
        const_in = sem("const_in")
        ctx_in = [sem("ctx_in0"), sem("ctx_in1")]
        mask_in = [sem("mask_in0"), sem("mask_in1")]
        ident_zero = sem("ident_zero")
        ident_ok = sem("ident_ok")
        b2_zero = sem("b2_zero")
        kT_zero = sem("kT_zero")
        ones_ok = sem("ones_ok")
        bias_T = sem("bias_T")
        bias_copied = sem("bias_copied")
        dve_step = sem("dve_step")
        dve_step2 = sem("dve_step2")
        std_ok = sem("std_ok")
        var_ok = sem("var_ok")
        q_ok = sem("q_ok")
        pool_hi = sem("pool_hi")
        stacked = sem("stacked")
        values_ok = sem("values_ok")
        aux_full = sem("aux_full")
        aux_read = sem("aux_read")
        scores = sem("scores")
        masked = sem("masked")
        exped = sem("exped")
        p_turned = sem("p_turned")
        pT_by_dve = sem("pT_by_dve")
        pT_by_act = sem("pT_by_act")
        pv_couples = sem("pv_couples")
        att_ok = sem("att_ok")
        x2_ok = sem("x2_ok")

        def waits_apart(eng, *waits):
            values = [eng.to_reg(v) for _, v in waits]
            eng.wait_ge(ident_ok, 1)
            for (s, _), v in zip(waits, values):
                eng.wait_ge(s, v)

        PT_BANK = 2
        AUX = 6
        CB_BANK = 7
        auxb = ps[:, AUX, :]
        ctx_ps = ps[0:S, CB_BANK, 0:HEADS * (DH + 1)].rearrange("s (h c) -> s h c", h=HEADS)

        def attention(block, sba):
            ctx_sb = sba("ctx_sb", [KP, 2, KT, D])
            mask_sb = sba("mask_sb", [S, 2, SK])
            kst = sba("kst", [KP, 2, KT, HEADS, 4, DH])
            qst = sba("qst", [S, 2, HEADS, 4, DH])
            vaug = sba("vaug", [KP, 2, KT, HEADS, DH + 1])
            kT = sba("kT", [P, 2, NKU, SKE], F32R)
            qT = sba("qT", [P, 2, HEADS // 2, S], F32R)
            nsm = sba("nsm", [S, 4, SK])
            nmax = sba("nmax", [S, 4])
            prob = sba("prob", [S, 4, SK])
            pT = sba("pT", [KP, 2, 2, KT * S])
            rsum = sba("rsum", [S, HEADS])
            att = sba("att", [S, D])
            attT = sba("attT", [P, DK, S])
            prj = sba("prj", [S, D])

            def one_of(t, b):
                return t[bass.ds(b, 1), :, :].rearrange("o a b -> (o a) b")

            @block.sync
            def _(sp):
                sp.dma_start(x_sb[:], x.rearrange("b s d -> s b d")).then_inc(x_in, 16)

                def load_context(b, par):
                    sp.dma_start(ctx_sb[:, par], one_of(ctx, b).rearrange("(t p) d -> p t d", p=KP)).then_inc(ctx_in[par], 16)

                def load_mask(b, par):
                    sp.dma_start(mask_sb[:, par], one_of(mask.rearrange("b o s k -> (b o) s k"), b)).then_inc(mask_in[par], 16)

                for b in range(2):
                    load_context(b, b)
                    load_mask(b, b)
                sp.dma_start(wo_raw[:], wo_w.rearrange("(t p) d -> p t d", p=P)).then_inc(const_in, 16)
                sp.dma_start(wob[:], wo_b.rearrange("(o d) -> o d", o=1).to_broadcast([S, D])).then_inc(const_in, 16)
                sp.dma_start(gw_sb[:], gw.rearrange("(t p) e -> p t e", p=P)).then_inc(const_in, 16)
                sp.dma_start(gb_sb[:], gb.rearrange("(o d) -> o d", o=1).to_broadcast([S, E])).then_inc(const_in, 16)
                sp.dma_start(b1r[0:E, :], b1).then_inc(const_in, 16)
                sp.dma_start(b1r[E:NE, :], sb1.rearrange("(t p) -> t p", p=P)).then_inc(const_in, 16)
                sp.dma_start(b3r[0:E, :], b3).then_inc(const_in, 16)
                sp.dma_start(b3r[E:NE, :], sb3.rearrange("(t p) -> t p", p=P)).then_inc(const_in, 16)
                sp.wait_ge(b2_zero, 1)
                sp.dma_start(b2a[0:E, :], b2).then_inc(const_in, 16)
                sp.dma_start(b2a[E:E + 1, :], sb2.rearrange("(o d) -> o d", o=1)).then_inc(const_in, 16)
                load_expert(sp, 0, w1[0], w3[0], w2[0])
                load_expert(sp, 1, w1[1], w3[1], w2[1])
                with sp.Fori(1, B // 2) as i:
                    for par in range(2):
                        sp.wait_ge(stacked, 4 * (2 * i + par - 1))
                        sp.wait_ge(values_ok, 2 * i + par - 1)
                        load_context(2 * i + par, par)
                        sp.wait_ge(masked, 2 * NCP * i - HEADS * (1 - par))
                        load_mask(2 * i + par, par)

            @block.gpsimd
            def _(pool):
                pool.memset(ident[:], 0.0).then_inc(ident_zero, 1)
                pool.wait_ge(ident_zero, 1)
                pool.affine_select(out=ident[:], in_=ident[:], compare_op=ALU.not_equal, fill=1.0, base=0,
                                   pattern=[[-1, P]], channel_multiplier=1).then_inc(ident_ok, 1)
                pool.memset(b2a[:], 0.0).then_inc(b2_zero, 1)
                pool.memset(kT[:].bitcast(F32), 0.0).then_inc(kT_zero, 1)
                pool.memset(vaug[:], 1.0).then_inc(ones_ok, 1)
                pool.wait_ge(ones_ok, 1)

                def pair(i, first):
                    for par in range(2):
                        b = 2 * i + par
                        kin = ctx_sb[:, par].rearrange("p t (h c) -> p (t h) c", c=DH)
                        kview = kst[:, par].rearrange("p t h f c -> p (t h) f c")
                        qin = q_sb[:, bass.ds(b, 1), :].rearrange("s o (h c) -> s (o h) c", c=DH)
                        qview = qst[:, par]
                        both = ((ctx_in[par], 16 * i + 16), (scores, 2 * NCP * (i - 1) + HEADS * par + 1))
                        waits_apart(pool, *both[:1 if first else 2])
                        for f in (0, 2):
                            pool.tensor_copy(kview[:, :, f, :].bitcast(F32R), kin).then_inc(pool_hi, 1)
                        if first and par == 0:
                            pool.wait_ge(q_ok, 1)
                        for f in (0, 1):
                            pool.tensor_copy(qview[:, :, f, :].bitcast(F32R), qin).then_inc(pool_hi, 1)
                        waits_apart(pool, (pool_hi, 4 * b + 4))
                        for f in (2, 3):
                            pool.tensor_tensor(qview[:, :, f, :], qin, qview[:, :, 0, :],
                                               ALU.subtract).then_inc(stacked, 1)
                        for f in (1, 3):
                            pool.tensor_tensor(kview[:, :, f, :], kin, kview[:, :, 0, :],
                                               ALU.subtract).then_inc(stacked, 1)
                        if not first:
                            waits_apart(pool, (pv_couples, NCP * i - CPB * (1 - par)))
                        pool.tensor_copy(vaug[:, par, :, :, 0:DH],
                                         ctx_sb[:, par].rearrange("p t (h c) -> p t h c", c=DH)
                                         ).then_inc(values_ok, 1)

                pair(0, True)
                with pool.Fori(1, B // 2) as i:
                    pair(i, False)

            def prep_fill(pe, n, b, par):
                if n == 0:
                    pe.wait_ge(stacked, 4 * b + 4)
                if n < NQU:
                    for g in range(4):
                        h2 = n * 4 + g
                        last = nc.tensor.transpose(auxb[:, g * S:(g + 1) * S],
                                                   qst[:, par, 2 * h2:2 * h2 + 2].rearrange("s h f c -> s (h f c)"),
                                                   ident[0:S, 0:S])
                else:
                    g = n - NQU
                    for t in range(KT):
                        last = nc.tensor.transpose(auxb[:, t * KP:(t + 1) * KP],
                                                   kst[:, par, t, 2 * g:2 * g + 2].rearrange("s h f c -> s (h f c)"),
                                                   ident[0:KP, 0:KP])
                last.then_inc(aux_full, 1)

            def prep_read(n, par):
                if n < NQU:
                    return (qT[:, par, 4 * n:4 * n + 4, :].rearrange("p g s -> p (g s)"), auxb[:, 0:4 * S])
                return kT[:, par, n - NQU, 0:SK], auxb[:, 0:SK]

            def aux_base(i):
                return NPREP + NAUX * i

            @block.tensor
            def _(pe):
                pe.wait_ge(ident_ok, 1)
                pe.wait_ge(const_in, 16 * 10)
                for t in range(DK):
                    for k in range(DK):
                        nc.tensor.transpose(ps[:, 0, (k * DK + t) * P:(k * DK + t + 1) * P],
                                            wo_raw[:, t, k * P:(k + 1) * P], ident[:])
                nc.tensor.transpose(ps[:, 1, 0:NE], b1r[:], ident[0:NE, 0:NE])
                nc.tensor.transpose(ps[:, 1, P:P + NE], b3r[:], ident[0:NE, 0:NE]).then_inc(bias_T, 1)
                pe.wait_ge(bias_copied, 3)
                for n in range(NPREP):
                    if n:
                        pe.wait_ge(aux_read, n)
                    prep_fill(pe, n, 0, 0)

                def pair(i, last):
                    plan = aux_plan(last)

                    def unit(j):
                        _, kind, n, half, _ = plan[j]
                        pe.wait_ge(aux_read, aux_base(i) + j)
                        if kind == "prep":
                            b, par = (2 * i + 1, 1) if half == 0 else (2 * i + 2, 0)
                            prep_fill(pe, n, b, par)
                            return
                        b = 2 * i + half
                        if kind == "ctxT":
                            pe.wait_ge(att_ok, b + 1)
                            for k in range(DK):
                                ins = nc.tensor.transpose(auxb[:, k * S:(k + 1) * S], att[:, k * P:(k + 1) * P],
                                                          ident[0:S, 0:S])
                        else:
                            for k in range(DK):
                                ins = nc.tensor.matmul(auxb[0:S, 0:D], attT[:, k, :], woT[:, k, :],
                                                       start=(k == 0), stop=(k == DK - 1))
                        ins.then_inc(aux_full, 1)

                    j = 0
                    for c in range(NCP + 4):
                        if c < NCP:
                            half = c // CPB
                            if c % CPB == 0:
                                pe.wait_ge(aux_read, aux_base(i) if half == 0 else
                                           aux_base(i) + max(k for k, u in enumerate(plan)
                                                             if u[1] == "prep" and u[3] == 0) + 1)
                            for n in (2 * c, 2 * c + 1):
                                h = n % HEADS
                                r = 64 * (h % 2)
                                pe.wait_ge(masked, 2 * NCP * i + max(0, n - 1))
                                nc.tensor.matmul(ps[0:S, n % 2, 0:SKE], qT[r:r + 64, half, h // 2, :],
                                                 kT[r:r + 64, half, h // 2, :], start=True, stop=True).then_inc(scores, 1)
                        if 1 <= c <= NCP:
                            d = c - 1
                            pe.wait_ge(exped, 2 * NCP * i + 2 * d + 2)
                            nd, na = counts(d - 1)
                            pe.wait_ge(pT_by_dve, D_PAIR * i + nd)
                            pe.wait_ge(pT_by_act, A_PAIR * i + na)
                            for m in range(2):
                                for t in range(KT):
                                    ins = nc.tensor.transpose(
                                        ps[0:KP, PT_BANK + 2 * (d % 2) + m, t * S:(t + 1) * S],
                                        prob[:, (2 * d + m) % 4, t * KP:(t + 1) * KP], ident[0:S, 0:S])
                            ins.then_inc(p_turned, 1)
                        if 2 <= c <= NCP + 1:
                            d = c - 2
                            nd, na = counts(d + 1)
                            pe.wait_ge(pT_by_dve, D_PAIR * i + nd)
                            pe.wait_ge(pT_by_act, A_PAIR * i + na)
                            if d % CPB == 0:
                                pe.wait_ge(att_ok, 2 * i + d // CPB)
                                pe.wait_ge(values_ok, 2 * i + d // CPB + 1)
                            for m in range(2):
                                h = (2 * d + m) % HEADS
                                for t in range(KT):
                                    ins = nc.tensor.matmul(ctx_ps[:, h, :], pT[:, d % 2, m, t * S:(t + 1) * S],
                                                           vaug[:, d // CPB, t, h, :],
                                                           start=(t == 0), stop=(t == KT - 1))
                            ins.then_inc(pv_couples, 1)
                        while j < len(plan) and plan[j][0] == c:
                            unit(j)
                            j += 1
                    assert j == len(plan)

                with pe.Fori(0, B // 2 - 1) as i:
                    pair(i, False)
                pair(B // 2 - 1, True)

            @block.scalar
            def _(act):
                act.wait_ge(var_ok, 1)
                nc.scalar.activation(std[:], veps[:], ACT.Sqrt).then_inc(std_ok, 1)
                act.wait_ge(bias_T, 1)
                nc.scalar.copy(b1T[:], ps[:, 1, 0:NE]).then_inc(bias_copied, 1)
                nc.scalar.copy(b3T[:], ps[:, 1, P:P + NE]).then_inc(bias_copied, 1)

                def read_prep(n, par):
                    dst, src = prep_read(n, par)
                    nc.scalar.copy(dst, src).then_inc(aux_read, 1)

                act.wait_ge(kT_zero, 1)
                for n in range(NPREP):
                    if n % 2 == 0:
                        act.wait_ge(aux_full, n + 1)
                        read_prep(n, 0)

                def pair(i, last):
                    plan = aux_plan(last)
                    j = 0
                    for c in range(NCP + 4):
                        if c < NCP:
                            for n in (2 * c, 2 * c + 1):
                                act.wait_ge(masked, 2 * NCP * i + n + 1)
                                act.wait_ge(p_turned, NCP * i + max(0, n // 2 - 1))
                                nc.scalar.activation(prob[:, n % 4, :], nsm[:, n % 4, :], ACT.Exp, scale=-1.0,
                                                     bias=nmax[:, n % 4:n % 4 + 1]).then_inc(exped, 1)
                        d = c - 1
                        if 0 <= d < NCP and not copied_by_dve(d):
                            act.wait_ge(p_turned, NCP * i + d + 1)
                            act.wait_ge(pv_couples, NCP * i + max(0, d - 1))
                            nc.scalar.copy(pT[:, d % 2], ps[0:KP, PT_BANK + 2 * (d % 2):PT_BANK + 2 * (d % 2) + 2,
                                                            0:KT * S]).then_inc(pT_by_act, 1)
                        while j < len(plan) and plan[j][0] == c:
                            _, kind, n, half, who = plan[j]
                            if who == "ACT":
                                act.wait_ge(aux_full, aux_base(i) + j + 1)
                                if kind == "prep":
                                    read_prep(n, 1 - half)
                                else:
                                    nc.scalar.copy(attT[:].rearrange("p k s -> p (k s)"),
                                                   auxb[:, 0:DK * S]).then_inc(aux_read, 1)
                            j += 1

                with act.Fori(0, B // 2 - 1) as i:
                    pair(i, False)
                pair(B // 2 - 1, True)

            @block.vector
            def _(dve):
                dve.wait_ge(x_in, 16)
                for b in range(B):
                    nc.vector.bn_stats(stats[:, b, :], x_sb[:, b, :]).then_inc(dve_step, 1)
                dve.wait_ge(dve_step, B)
                for b in range(B):
                    nc.vector.bn_aggr(mv[:, b, :], stats[:, b, :]).then_inc(dve_step, 1)
                dve.wait_ge(dve_step, 2 * B)
                nc.vector.tensor_scalar(veps[:], mv[:, :, 1], EPS, None, ALU.add).then_inc(var_ok, 1)
                dve.wait_ge(std_ok, 1)
                nc.vector.reciprocal(rstd[:], std[:]).then_inc(dve_step, 1)
                dve.wait_ge(dve_step, 2 * B + 1)
                for b in range(B):
                    ins = nc.vector.tensor_scalar(q_sb[:, b, :], x_sb[:, b, :], mv[:, b, 0:1], rstd[:, b:b + 1],
                                                  ALU.subtract, ALU.mult)
                ins.then_inc(q_ok, 1)
                dve.wait_ge(bias_T, 1)
                nc.vector.tensor_copy(woT[:].rearrange("p k d -> p (k d)"), ps[:, 0, :]).then_inc(bias_copied, 1)

                def read_prep(n, par):
                    dst, src = prep_read(n, par)
                    nc.vector.tensor_copy(dst, src).then_inc(aux_read, 1)

                dve.wait_ge(kT_zero, 1)
                for n in range(NPREP):
                    if n % 2 == 1:
                        dve.wait_ge(aux_full, n + 1)
                        read_prep(n, 0)
                STEP0 = 2 * B + 1
                TAIL_STEPS = 3

                def pair(i, last):
                    plan = aux_plan(last)
                    j = 0
                    for c in range(NCP + 4):
                        if c < NCP:
                            half = c // CPB
                            if c % CPB == 0:
                                dve.wait_ge(mask_in[half], 16 * i + 16)
                            for n in (2 * c, 2 * c + 1):
                                both = ((scores, 2 * NCP * i + n + 1), (exped, 2 * NCP * i + max(0, n - 3)))
                                waits_apart(dve, *both)
                                nc.vector.tensor_tensor_reduce(
                                    out=nsm[:, n % 4, :], in0=ps[0:S, n % 2, 0:SK], in1=mask_sb[:, half, :],
                                    scale=-1.0, scalar=BIG, op0=ALU.add, op1=ALU.min,
                                    accum_out=nmax[:, n % 4:n % 4 + 1]).then_inc(masked, 1)
                        d = c - 1
                        if 0 <= d < NCP and copied_by_dve(d):
                            dve.wait_ge(p_turned, NCP * i + d + 1)
                            dve.wait_ge(pv_couples, NCP * i + max(0, d - 1))
                            nc.vector.tensor_copy(pT[:, d % 2], ps[0:KP, PT_BANK + 2 * (d % 2):PT_BANK + 2 * (d % 2) + 2,
                                                                   0:KT * S]).then_inc(pT_by_dve, 1)
                        if c in (CPB + 1, NCP + 1):
                            half = c // CPB - 1
                            b = 2 * i + half
                            s0 = STEP0 + TAIL_STEPS * b
                            dve.wait_ge(pv_couples, NCP * i + CPB * (half + 1))
                            nc.vector.reciprocal(rsum[:], ctx_ps[:, :, DH]).then_inc(dve_step, 1)
                            dve.wait_ge(dve_step, s0 + 1)
                            nc.vector.tensor_tensor(att[:].rearrange("s (h c) -> s h c", c=DH), ctx_ps[:, :, 0:DH],
                                                    rsum[:].unsqueeze(2).to_broadcast([S, HEADS, DH]),
                                                    ALU.mult).then_inc(att_ok, 1)
                        while j < len(plan) and plan[j][0] == c:
                            _, kind, n, half, who = plan[j]
                            if who == "DVE":
                                dve.wait_ge(aux_full, aux_base(i) + j + 1)
                                if kind == "prep":
                                    read_prep(n, 1 - half)
                                else:
                                    b = 2 * i + half
                                    s0 = STEP0 + TAIL_STEPS * b
                                    xb = x_sb[:, bass.ds(b, 1), :].rearrange("s o d -> s (o d)")
                                    x2b = x2[:, bass.ds(b, 1), :].rearrange("s o d -> s (o d)")
                                    nc.vector.tensor_tensor(prj[:], auxb[0:S, 0:D], wob[:], ALU.add).then_inc(aux_read, 1)
                                    dve.wait_ge(aux_read, aux_base(i) + j + 1)
                                    nc.vector.scalar_tensor_tensor(x2b, prj[:], 0.0, xb, ALU.max,
                                                                   ALU.add).then_inc(dve_step, 1)
                                    dve.wait_ge(dve_step, s0 + 2)
                                    nc.vector.bn_stats(stats[:, bass.ds(b, 1), :].rearrange("s o d -> s (o d)"),
                                                       x2b).then_inc(dve_step, 1)
                            j += 1

                with dve.Fori(0, B // 2 - 1) as i:
                    pair(i, False)
                pair(B // 2 - 1, True)



        w_in = [sem("w_in0"), sem("w_in1")]
        gate_in = [sem("gate_in0"), sem("gate_in1")]
        gate_out = sem("gate_out")
        xn_ok = sem("xn_ok")
        xT_full = sem("xT_full")
        xf_ok = sem("xf_ok")
        xhi_ok = sem("xhi_ok")
        xlo_ok = sem("xlo_ok")
        logits_ok = sem("logits_ok")
        lmax_ok = sem("lmax_ok")
        probs_ok = sem("probs_ok")
        cw_ok = sem("cw_ok")
        cw_turned = sem("cw_turned")
        cwT_ok = sem("cwT_ok")
        const_ok = sem("const_ok")
        whi_ok = sem("whi_ok")
        wlo_ok = sem("wlo_ok")
        h1_full = sem("h1_full")
        h3_full = sem("h3_full")
        silu_ok = sem("silu_ok")
        gated = sem("gated")
        h_ok = sem("h_ok")
        hhi_ok = sem("hhi_ok")
        hlo_ok = sem("hlo_ok")
        down_done = sem("down_done")
        y_by_act = sem("y_by_act")
        y_by_dve = sem("y_by_dve")
        y_turned = sem("y_turned")
        out_ok = sem("out_ok")
        out_sent = sem("out_sent")
        std2_ok = sem("std2_ok")
        var2_ok = sem("var2_ok")

        def load_expert(sp, slot, a1, a3, a2):
            sp.dma_start(wr[:, slot, 0:DK, 0:INTER], a1.rearrange("(k p) i -> p k i", p=P)).then_inc(w_in[slot], 16)
            sp.dma_start(wr[:, slot, 0:DK, INTER:D], a3.rearrange("(k p) i -> p k i", p=P)).then_inc(w_in[slot], 16)
            sp.dma_start(wr[:, slot, DK, :], a2).then_inc(w_in[slot], 16)

        def experts(block, sbe):
            xn = sbe("xn", [S, B, D])
            xf = sbe("xf", [P, DK, T])
            xhi = sbe("xhi", [P, DK, T], F32R)
            xlo = sbe("xlo", [P, DK, T], F32R)
            whi = sbe("whi", [P, 2, 3, D], F32R)
            wlo = sbe("wlo", [P, 2, 3, D], F32R)
            lg = sbe("lg", [S, B, E])
            lmax = sbe("lmax", [S, B])
            ld = sbe("ld", [S, B, E])
            ex = sbe("ex", [S, B, E])
            esum = sbe("esum", [S, B])
            sc = sbe("sc", [S, B, E])
            pmax = sbe("pmax", [S, B * GROUPS, 2])
            pmin = sbe("pmin", [S, B * GROUPS, 2])
            top1 = sbe("top1", [S, B * GROUPS])
            lowm = sbe("lowm", [S, B * GROUPS])
            highm = sbe("highm", [S, B * GROUPS])
            top2 = sbe("top2", [S, B * GROUPS])
            gs = sbe("gs", [S, B, GROUPS])
            keep = sbe("keep", [S, B, GROUPS])
            keepm = sbe("keepm", [S, B, GROUPS])
            msc = sbe("msc", [S, B, E])
            sel = sbe("sel", [S, B, E])
            best = sbe("best", [S, B, 8])
            above = sbe("above", [S, B, E])
            equal = sbe("equal", [S, B, E])
            naabove = sbe("naabove", [S, B])
            prefix = sbe("prefix", [S, B, E])
            restart = sbe("restart", [S, B, E])
            restart_g = sbe("restart_g", [S, B, GROUPS])
            cw = sbe("cw", [S, B, NE])
            cwT = sbe("cwT", [NE, T])
            we = sbe("we", [P, 2, T])
            sil = sbe("sil", [P, 2, CT])
            tg = sbe("tg", [P, 2, CT])
            hf = sbe("hf", [P, 2, CT])
            hhi = sbe("hhi", [P, 2, CT], F32R)
            hlo = sbe("hlo", [P, 2, CT], F32R)
            yT = sbe("yT", [P, DK, T])
            o_sb = sbe("o_sb", [S, B, D])

            def up_ps(which, par):
                return ps[:, 2 * par + which, 0:CT]

            def y_ps(k, c):
                return ps[:, 4 + 2 * k + c, 0:CT]

            NU = 2 * NE
            NPAIR = NE // 2

            @block.sync
            def _(sp):
                def gate_row(e, slot):
                    sp.dma_start(we[:, slot, :], scratch[bass.ds(e, 1), :].to_broadcast([P, T])).then_inc(gate_in[slot], 16)

                for c in range(NCH):
                    sp.wait_ge(cwT_ok, c + 1)
                    sp.dma_start(scratch[:, c * CT:(c + 1) * CT], cwT[:, c * CT:(c + 1) * CT]).then_inc(gate_out, 16)
                sp.wait_ge(gate_out, 16 * NCH)
                gate_row(0, 0)
                gate_row(1, 1)

                def refill(e, slot, shared):
                    sp.wait_ge(whi_ok, e - 1)
                    sp.wait_ge(wlo_ok, e - 1)
                    if shared:
                        cols = slice(slot * INTER, (slot + 1) * INTER)
                        load_expert(sp, slot, sw1[:, cols], sw3[:, cols], sw2[cols, :])
                    else:
                        load_expert(sp, slot, one(w1, e), one(w3, e), one(w2, e))
                    sp.wait_ge(gated, 2 * (e - 1))
                    gate_row(e, slot)

                def one(w, e):
                    return w[bass.ds(e, 1), :, :].rearrange("o a b -> (o a) b")

                with sp.Fori(1, NPAIR - 1) as i:
                    for slot in range(2):
                        refill(2 * i + slot, slot, False)
                for slot in range(2):
                    refill(E + slot, slot, True)

                for q in range(B // 2):
                    sp.wait_ge(out_ok, 2 * q + 2)
                    sp.dma_start(out[2 * q:2 * q + 2].rearrange("b s d -> s b d"),
                                 o_sb[:, 2 * q:2 * q + 2, :]).then_inc(out_sent, 16)
                sp.wait_ge(out_sent, 16 * (B // 2))

            @block.gpsimd
            def _(pool):
                pool.memset(restart[:], 1.0).then_inc(const_ok, 1)
                pool.memset(restart_g[:], 1.0).then_inc(const_ok, 1)
                pool.memset(cw[:], 1.0).then_inc(const_ok, 1)
                pool.wait_ge(const_ok, 3)
                pool.memset(restart[:, :, 0:1], 0.0).then_inc(const_ok, 1)
                pool.memset(restart_g[:, :, 0:1], 0.0).then_inc(const_ok, 1)

            @block.tensor
            def _(pe):
                pe.wait_ge(xn_ok, 1)
                for c in range(NCH):
                    for k in range(DK):
                        for b in range(CB):
                            ins = nc.tensor.transpose(ps[:, 2 * c + k, b * S:(b + 1) * S],
                                                      xn[:, c * CB + b, k * P:(k + 1) * P], ident[0:S, 0:S])
                        ins.then_inc(xT_full, 1)
                pe.wait_ge(xf_ok, 2 * NCH)
                for b in range(B):
                    for k in range(DK):
                        ins = nc.tensor.matmul(ps[0:S, 4, b * E:(b + 1) * E], xf[:, k, b * S:(b + 1) * S],
                                               gw_sb[:, k, :], start=(k == 0), stop=(k == DK - 1))
                ins.then_inc(logits_ok, 1)

                pe.wait_ge(xhi_ok, 2 * NCH)
                pe.wait_ge(xlo_ok, 2 * NCH)

                def up(u, e, slot, c):
                    if c == 0:
                        pe.wait_ge(whi_ok, e + 1)
                        pe.wait_ge(wlo_ok, e + 1)
                    par = c
                    for which, full, read in ((0, h1_full, silu_ok), (1, h3_full, h_ok)):
                        if u is not None:
                            pe.wait_ge(read, u - 1)
                        n = 0
                        cols = slice(which * INTER, (which + 1) * INTER)
                        for k in range(DK):
                            toks = slice(c * CT, (c + 1) * CT)
                            for wt, xt in ((whi, xhi), (whi, xlo), (wlo, xhi)):
                                ins = nc.tensor.matmul(up_ps(which, par), wt[:, slot, k, cols], xt[:, k, toks],
                                                       start=(n == 0), stop=(n == 3 * DK - 1))
                                n += 1
                        ins.then_inc(full, 1)

                def down(u, slot, c, last=False):
                    pe.wait_ge(hhi_ok, u + 1)
                    order = [(whi, hhi, k) for k in range(DK)] + [(wlo, hhi, k) for k in range(DK)]
                    order += [(whi, hlo, k) for k in range(DK)]
                    for n, (wt, ht, k) in enumerate(order):
                        if n == 2 * DK:
                            pe.wait_ge(hlo_ok, u + 1)
                        ins = nc.tensor.matmul(y_ps(k, c), wt[:, slot, DK, k * P:(k + 1) * P], ht[:, c, :],
                                               start=False, stop=last and n >= 2 * DK, skip_group_check=True)
                    ins.then_inc(down_done, 1)

                up(None, 0, 0, 0)
                pe.wait_ge(cw_ok, 1)
                for c in range(NCH):
                    for b in range(CB):
                        ins = nc.tensor.transpose(ps[0:NE, 2 + c, b * S:(b + 1) * S], cw[:, c * CB + b, :],
                                                  ident[0:S, 0:S])
                    ins.then_inc(cw_turned, 1)
                pe.wait_ge(cwT_ok, NCH)
                for c in range(NCH):
                    for k in range(DK):
                        nc.tensor.matmul(y_ps(k, c), b2a[:, k * P:(k + 1) * P], cwT[:, c * CT:(c + 1) * CT],
                                         start=True, stop=False, skip_group_check=True)
                up(None, 0, 0, 1)
                down(0, 0, 0)
                up(2, 1, 1, 0)
                down(1, 0, 1)
                up(3, 1, 1, 1)
                down(2, 1, 0)

                with pe.Fori(1, NPAIR) as i:
                    up(4 * i, 2 * i, 0, 0)
                    down(4 * i - 1, 1, 1)
                    up(4 * i + 1, 2 * i, 0, 1)
                    down(4 * i, 0, 0)
                    up(4 * i + 2, 2 * i + 1, 1, 0)
                    down(4 * i + 1, 0, 1)
                    up(4 * i + 3, 2 * i + 1, 1, 1)
                    down(4 * i + 2, 1, 0)
                down(NU - 1, 1, 1, True)

                for b in range(B):
                    c = b // CB
                    if b % CB == 0:
                        pe.wait_ge(y_by_act, c + 1)
                        pe.wait_ge(y_by_dve, c + 1)
                    for k in range(DK):
                        ins = nc.tensor.transpose(ps[0:S, b // 2, (b % 2) * D + k * P:(b % 2) * D + (k + 1) * P],
                                                  yT[:, k, b * S:(b + 1) * S], ident[:])
                    ins.then_inc(y_turned, 1)

            @block.scalar
            def _(act):
                act.wait_ge(var2_ok, 1)
                nc.scalar.activation(std[:], veps[:], ACT.Sqrt).then_inc(std2_ok, 1)
                for n in range(2 * NCH):
                    c, k = n // DK, n % DK
                    act.wait_ge(xT_full, n + 1)
                    nc.scalar.copy(xf[:, k, c * CT:(c + 1) * CT], ps[:, n, 0:CT]).then_inc(xf_ok, 1)
                    nc.scalar.copy(xhi[:, k, c * CT:(c + 1) * CT], ps[:, n, 0:CT]).then_inc(xhi_ok, 1)
                act.wait_ge(lmax_ok, 1)
                nc.scalar.activation(ex[:], ld[:], ACT.Exp).then_inc(probs_ok, 1)

                def split_hi(e, slot, n):
                    act.wait_ge(w_in[slot], 48 * (n + 1))
                    if e is not None:
                        act.wait_ge(down_done, 2 * e - 2)
                        act.wait_ge(wlo_ok, e - 1)
                    nc.scalar.copy(whi[:, slot].rearrange("p k d -> p (k d)"),
                                   wr[:, slot].rearrange("p k d -> p (k d)")).then_inc(whi_ok, 1)

                def silu(u, e, c):
                    waits_apart(act, (h1_full, u + 1))
                    nc.scalar.activation(sil[:, c, :], up_ps(0, c), ACT.Silu,
                                         bias=b1T[:, bass.ds(e, 1)]).then_inc(silu_ok, 1)

                def hi(u, c):
                    act.wait_ge(h_ok, u + 1)
                    nc.scalar.copy(hhi[:, c, :], hf[:, c, :]).then_inc(hhi_ok, 1)

                split_hi(None, 0, 0)
                split_hi(None, 1, 0)

                def pair(i, last, first=False):
                    for s in range(2):
                        e = 2 * i + s
                        for c in range(2):
                            u = 2 * e + c
                            silu(u, e, c)
                            if c == 1 and not (s == 0 and first) and not (last and s == 1):
                                nx = e + 1
                                split_hi(nx, 1 - s, i if s == 0 else i + 1)
                            hi(u, c)

                pair(0, False, True)
                with act.Fori(1, NPAIR - 1) as i:
                    pair(i, False)
                pair(NPAIR - 1, True)
                for n in range(2 * NCH):
                    c, k = n // DK, n % DK
                    if n % 2 == 0:
                        act.wait_ge(down_done, NU - 1 + c)
                        nc.scalar.copy(yT[:, k, c * CT:(c + 1) * CT], y_ps(k, c)).then_inc(y_by_act, 1)

            @block.vector
            def _(dve):
                steps = {"n": 0}

                def chained(ins):
                    steps["n"] += 1
                    ins.then_inc(gate_step, 1)
                    dve.wait_ge(gate_step, steps["n"])

                gate_step = dve_step2
                TT = nc.vector.tensor_tensor
                for b in range(B):
                    ins = nc.vector.bn_aggr(mv[:, b, :], stats[:, b, :])
                chained(ins)
                nc.vector.tensor_scalar(veps[:], mv[:, :, 1], EPS, None, ALU.add).then_inc(var2_ok, 1)
                dve.wait_ge(std2_ok, 1)
                chained(nc.vector.reciprocal(rstd[:], std[:]))
                for b in range(B):
                    ins = nc.vector.tensor_scalar(xn[:, b, :], x2[:, b, :], mv[:, b, 0:1], rstd[:, b:b + 1],
                                                  ALU.subtract, ALU.mult)
                ins.then_inc(xn_ok, 1)
                for n in range(2 * NCH):
                    c, k = n // DK, n % DK
                    toks = slice(c * CT, (c + 1) * CT)
                    dve.wait_ge(xf_ok, n + 1)
                    dve.wait_ge(xhi_ok, n + 1)
                    TT(xlo[:, k, toks], xf[:, k, toks], xhi[:, k, toks].bitcast(F32), ALU.subtract).then_inc(xlo_ok, 1)

                def split_lo(e, slot, n):
                    dve.wait_ge(whi_ok, e + 1)
                    TT(wlo[:, slot].rearrange("p k d -> p (k d)"), wr[:, slot].rearrange("p k d -> p (k d)"),
                       whi[:, slot].rearrange("p k d -> p (k d)").bitcast(F32), ALU.subtract).then_inc(wlo_ok, 1)

                def over(ap, shape):
                    return ap.unsqueeze(2).to_broadcast(shape)

                dve.wait_ge(logits_ok, 1)
                chained(TT(lg[:], ps[0:S, 4, 0:B * E].rearrange("s (b e) -> s b e", e=E),
                           gb_sb[:].unsqueeze(1).to_broadcast([S, B, E]), ALU.add))
                chained(nc.vector.tensor_reduce(lmax[:], lg[:], AX.X, ALU.max))
                TT(ld[:], lg[:], over(lmax[:], [S, B, E]), ALU.subtract).then_inc(lmax_ok, 1)
                dve.wait_ge(probs_ok, 1)
                chained(nc.vector.tensor_reduce(esum[:], ex[:], AX.X, ALU.add))
                chained(nc.vector.reciprocal(lmax[:], esum[:]))
                chained(TT(sc[:], ex[:], over(lmax[:], [S, B, E]), ALU.mult))
                four = sc[:].rearrange("s b (g f) -> s (b g) f", f=GE)
                nc.vector.tensor_tensor(pmax[:], four[:, :, 0:2], four[:, :, 2:4], ALU.max)
                chained(TT(pmin[:], four[:, :, 0:2], four[:, :, 2:4], ALU.min))
                TT(top1[:], pmax[:, :, 0], pmax[:, :, 1], ALU.max)
                TT(lowm[:], pmax[:, :, 0], pmax[:, :, 1], ALU.min)
                chained(TT(highm[:], pmin[:, :, 0], pmin[:, :, 1], ALU.max))
                chained(TT(top2[:], lowm[:], highm[:], ALU.max))
                chained(TT(gs[:].rearrange("s b g -> s (b g)"), top1[:], top2[:], ALU.add))

                def choose(chosen, values, width, count, starts):
                    for b in range(B):
                        ins = nc.vector.max(best[:, b, :], values[:, b, :])
                    chained(ins)
                    lim = best[:, :, count - 1:count].to_broadcast([S, B, width])
                    ab, eq, pf = above[:, :, 0:width], equal[:, :, 0:width], prefix
                    if width != E:
                        ab = above[:].rearrange("s b e -> s (b e)")[:, 0:B * width].rearrange("s (b w) -> s b w", w=width)
                        eq = equal[:].rearrange("s b e -> s (b e)")[:, 0:B * width].rearrange("s (b w) -> s b w", w=width)
                    pf = prefix[:].rearrange("s b e -> s (b e)")[:, 0:B * width]
                    TT(ab, values, lim, ALU.is_gt)
                    chained(TT(eq, values, lim, ALU.is_equal))
                    nc.vector.tensor_reduce(naabove[:], ab, AX.X, ALU.add)
                    chained(nc.vector.tensor_tensor_scan(pf, starts[:].rearrange("s b w -> s (b w)"),
                                                         eq.rearrange("s b w -> s (b w)"), 0.0, ALU.mult, ALU.add))
                    pf3 = pf.rearrange("s (b w) -> s b w", w=width)
                    chained(TT(pf3, pf3, over(naabove[:], [S, B, width]), ALU.add))
                    chained(nc.vector.scalar_tensor_tensor(eq, pf3, float(count), eq, ALU.is_le, ALU.mult))
                    chained(TT(chosen, ab, eq, ALU.add))

                dve.wait_ge(const_ok, 5)
                choose(keep[:], gs[:], GROUPS, KEEP_GROUPS, restart_g)
                chained(nc.vector.tensor_scalar(keepm[:], keep[:], -1.0, None, ALU.add))
                k4 = keep[:].rearrange("s b g -> s (b g)").unsqueeze(2).to_broadcast([S, B * GROUPS, GE])
                km4 = keepm[:].rearrange("s b g -> s (b g)").unsqueeze(2).to_broadcast([S, B * GROUPS, GE])
                m4 = msc[:].rearrange("s b (g f) -> s (b g) f", f=GE)
                chained(TT(m4, four, k4, ALU.mult))
                chained(TT(m4, m4, km4, ALU.add))
                choose(sel[:], msc[:], E, TOPK, restart)
                TT(cw[:, :, 0:E], sc[:], sel[:], ALU.mult).then_inc(cw_ok, 1)
                split_lo(0, 0, 0)
                split_lo(1, 1, 0)
                for c in range(NCH):
                    dve.wait_ge(cw_turned, c + 1)
                    nc.vector.tensor_copy(cwT[:, c * CT:(c + 1) * CT], ps[0:NE, 2 + c, 0:CT]).then_inc(cwT_ok, 1)

                def unit_gate(u, slot, c, n):
                    dve.wait_ge(silu_ok, u + 1)
                    dve.wait_ge(gate_in[slot], 16 * (n + 1))
                    TT(tg[:, c, :], sil[:, c, :], we[:, slot, c * CT:(c + 1) * CT], ALU.mult).then_inc(gated, 1)

                def unit_h(u, e, c):
                    dve.wait_ge(h3_full, u + 1)
                    dve.wait_ge(gated, u + 1)
                    nc.vector.scalar_tensor_tensor(hf[:, c, :], up_ps(1, c), b3T[:, bass.ds(e, 1)], tg[:, c, :],
                                                   ALU.add, ALU.mult).then_inc(h_ok, 1)

                def unit_lo(u, c):
                    dve.wait_ge(hhi_ok, u + 1)
                    TT(hlo[:, c, :], hf[:, c, :], hhi[:, c, :].bitcast(F32), ALU.subtract).then_inc(hlo_ok, 1)

                def pair(i, last, first=False):
                    for s in range(2):
                        e = 2 * i + s
                        for c in range(2):
                            u = 2 * e + c
                            unit_gate(u, s, c, i)
                            unit_h(u, e, c)
                            unit_lo(u, c)
                            if c == 1 and not (s == 0 and first) and not (last and s == 1):
                                split_lo(e + 1, 1 - s, None)

                pair(0, False, True)
                with dve.Fori(1, NPAIR - 1) as i:
                    pair(i, False)
                pair(NPAIR - 1, True)
                for n in range(2 * NCH):
                    c, k = n // DK, n % DK
                    if n % 2 == 1:
                        dve.wait_ge(down_done, NU - 1 + c)
                        nc.vector.tensor_copy(yT[:, k, c * CT:(c + 1) * CT], y_ps(k, c)).then_inc(y_by_dve, 1)
                for b in range(B):
                    dve.wait_ge(y_turned, 2 * (b // 2) + 2)
                    TT(o_sb[:, b, :], ps[0:S, b // 2, (b % 2) * D:(b % 2 + 1) * D], x2[:, b, :], ALU.add).then_inc(out_ok, 1)

        with ExitStack() as own:
            attention(own.enter_context(nc.Block()), lambda n, s, d=F32: own.enter_context(nc.sbuf_tensor(n, s, d)))
        with ExitStack() as own:
            experts(own.enter_context(nc.Block()), lambda n, s, d=F32: own.enter_context(nc.sbuf_tensor(n, s, d)))


_INS = ["x", "ctx_1024", "mask_Bx1xSxS2_ff0", "L0_xattn_wo_w", "L0_xattn_wo_b", "L0_ffn_gw", "L0_ffn_gb",
        "L0_ffn_w1", "L0_ffn_b1", "L0_ffn_w3", "L0_ffn_b3", "L0_ffn_w2", "L0_ffn_b2", "L0_ffn_sw1",
        "L0_ffn_sb1", "L0_ffn_sw3", "L0_ffn_sb3", "L0_ffn_sw2", "L0_ffn_sb2"]


def kernel(**inputs):
    import numpy as _np
    import concourse.bacc as _bacc
    from concourse import mybir as _mybir
    from concourse.bass_utils import run_bass_kernel_spmd as _run

    nc = _bacc.Bacc("TRN2", target_bir_lowering=False, num_devices=1)
    arrays, args = {}, []
    for name in _INS:
        a = _np.ascontiguousarray(inputs[name])
        arrays[f"in_{name}"] = a
        args.append(nc.dram_tensor(f"in_{name}", a.shape, _mybir.dt.from_np(a.dtype), kind="ExternalInput").ap())
    shape = inputs["x"].shape
    args.append(nc.dram_tensor("out_x", shape, _mybir.dt.float32, kind="ExternalOutput").ap())
    xattn_moe_kernel(nc, *args)
    r = _run(nc, [arrays], core_ids=[0])
    return r.results[0]["out_x"]
```

```python
from contextlib import ExitStack

import concourse.bass as bass
from concourse import mybir

ALU = mybir.AluOpType
ACT = mybir.ActivationFunctionType
AX = mybir.AxisListType
F32 = mybir.dt.float32
F32R = mybir.dt.float32r

P = 128
BANK = 512
HEADS = 16
TOPK = 4
KEEP_GROUPS = 4
GROUPS = 8
EPS = 1e-5
BIG = 3.0e38


def xattn_moe_kernel(nc, x, ctx, mask, wo_w, wo_b, gw, gb, w1, b1, w3, b3, w2, b2,
                     sw1, sb1, sw3, sb3, sw2, sb2, out):
    B, S, D = x.shape
    SK = ctx.shape[1]
    SKE = SK + SK % 2
    KT = 3
    KP = SK // KT
    DH = D // HEADS
    DK = D // P
    E, _, INTER = w1.shape
    VC = 32
    NSH = sw1.shape[1] // INTER
    NE = E + NSH
    GE = E // GROUPS
    T = B * S
    NCH = 2
    CB = B // NCH
    CT = CB * S
    assert KP * KT == SK and INTER == P and DK == 2 and DH == 16 and NSH == 2 and CT <= BANK and B % 2 == 0

    NH = 2 * HEADS
    T_LAG, C_LAG, PV_LAG = 3, 3, 5
    RING = 8
    SR, TR = 2, 2
    PR = 4
    NKU = HEADS // 2
    NQU = 2
    NPREP = NKU + NQU
    PREP_AT = [0, 1, 2, 3, 5, 7, 9, 11, 12, 13]
    DRAIN_AT = PV_LAG - 1
    TAIL = (("turn", 2, "DVE"), ("ctxT", 4, "ACT"), ("proj", 6, "DVE"))

    def aux_plan(first, last):
        plan = []
        for half in range(2):
            if half == 0 or not last:
                for n, at in enumerate(PREP_AT):
                    plan.append((half * HEADS + at, "prep", n, half + 1, "DVE" if n % 2 else "ACT"))
        for ends in ([] if first else [0]) + [HEADS] + ([NH] if last else []):
            for kind, later, who in TAIL:
                plan.append((ends + DRAIN_AT + later, kind, 0, ends // HEADS - 1, who))
        plan.sort(key=lambda u: u[0])
        return plan

    NAUX = len(aux_plan(False, False))

    def aux_base(i):
        return NPREP if isinstance(i, int) and i == 0 else NPREP + NAUX * i - len(TAIL)

    def aux_bank(i, j):
        return (aux_base(0 if isinstance(i, int) and i == 0 else 1) + j) % 2

    def aux_reads(i, plan, m):
        full = [u[4] for u in aux_plan(False, False)]
        pair_d, pair_a = full.count("DVE"), full.count("ACT")
        assert pair_d + pair_a == NAUX and NAUX % 2 == 0 and full[-1] == "DVE"
        own = [u[4] for u in plan[:max(0, m)]]
        if isinstance(i, int) and i == 0:
            d, a = NPREP // 2, NPREP // 2
        else:
            late = [u[2] for u in TAIL]
            d, a = NPREP // 2 + pair_d * i - late.count("DVE"), NPREP // 2 + pair_a * i - late.count("ACT")
        return d + own.count("DVE") - (m < 0), a + own.count("ACT")

    def copied_by_dve(n):
        return n % 8 in (0, 2, 4, 6, 7)

    def copies(n):
        d = sum(copied_by_dve(k) for k in range(n)) if n >= 0 else -sum(copied_by_dve(k) for k in range(n, 0))
        return d, n - d

    D_PAIR, A_PAIR = copies(NH)
    NSTEPS = NH + DRAIN_AT + TAIL[-1][1] + 1

    def wait(eng, s, value):
        if not isinstance(value, int) or value > 0:
            eng.wait_ge(s, value)

    scratch = nc.dram_tensor("gate_rows", (NE, T), F32, kind="Internal").ap()

    with ExitStack() as st:
        def sb(name, shape, dt=F32):
            return st.enter_context(nc.sbuf_tensor(name, shape, dt))

        def sem(name):
            return st.enter_context(nc.semaphore(name))

        ps = st.enter_context(nc.psum_tensor("ps", [P, 8, BANK], F32))

        ident = sb("ident", [P, P])
        x_sb = sb("x_sb", [S, B, D])
        q_sb = sb("q_sb", [S, B, D])
        x2 = sb("x2", [S, B, D])
        wo_raw = sb("wo_raw", [P, DK, D])
        woT = sb("woT", [P, DK, D])
        wob = sb("wob", [S, D])
        gw_sb = sb("gw_sb", [P, DK, E])
        gb_sb = sb("gb_sb", [S, E])
        b1r = sb("b1r", [NE, P])
        b3r = sb("b3r", [NE, P])
        b1T = sb("b1T", [P, NE])
        b3T = sb("b3T", [P, NE])
        b2a = sb("b2a", [NE, D])
        stats = sb("stats", [S, B, 6])
        mv = sb("mv", [S, B, 2])
        veps = sb("veps", [S, B])
        std = sb("std", [S, B])
        rstd = sb("rstd", [S, B])
        wr = sb("wr", [P, 2, 3, D])
        x_in = sem("x_in")
        const_in = sem("const_in")
        ctx_in = [sem("ctx_in0"), sem("ctx_in1")]
        mask_in = [sem("mask_in0"), sem("mask_in1")]
        ident_zero = sem("ident_zero")
        ident_ok = sem("ident_ok")
        identr_ok = sem("identr_ok")
        b2_zero = sem("b2_zero")
        kT_zero = sem("kT_zero")
        kst_zero = sem("kst_zero")
        values_zero = sem("values_zero")
        ones_ok = sem("ones_ok")
        bias_T = sem("bias_T")
        bias_copied = sem("bias_copied")
        dve_step = sem("dve_step")
        dve_step2 = sem("dve_step2")
        std_ok = sem("std_ok")
        var_ok = sem("var_ok")
        q_ok = sem("q_ok")
        pool_hi = sem("pool_hi")
        stacked = sem("stacked")
        values_ok = sem("values_ok")
        aux_full = sem("aux_full")
        aux_by_dve = sem("aux_by_dve")
        aux_by_act = sem("aux_by_act")
        scores = sem("scores")
        masked = sem("masked")
        exped = sem("exped")
        p_turned = sem("p_turned")
        pT_by_dve = sem("pT_by_dve")
        pT_by_act = sem("pT_by_act")
        pv_done = sem("pv_done")
        sums_ok = sem("sums_ok")
        rsum_ok = sem("rsum_ok")
        prj_ok = sem("prj_ok")
        x2_ok = sem("x2_ok")

        def waits_apart(eng, *waits):
            values = [eng.to_reg(v) for _, v in waits]
            eng.wait_ge(ident_ok, 1)
            for (s, _), v in zip(waits, values):
                eng.wait_ge(s, v)

        PT_BANK = SR
        AUX = SR + TR
        SUM_BANK = AUX + 2
        assert SUM_BANK + 2 == 8

        def attention(block, sba):
            ctx_sb = sba("ctx_sb", [KP, 2, KT, D])
            mask_sb = sba("mask_sb", [S, 2, SK])
            KPE = KP + KP % 2
            kst = sba("kst", [KPE, 2, KT, HEADS, 4, DH], F32R)
            qst = sba("qst", [S, 2, HEADS, 4, DH], F32R)
            identr = sba("identr", [P, P], F32R)
            vaug = sba("vaug", [KP, 2, KT, HEADS, VC])
            kT = sba("kT", [P, 2, NKU, SKE], F32R)
            qT = sba("qT", [P, 2, HEADS // 2, S], F32R)
            nsm = sba("nsm", [S, RING, SK])
            nmax = sba("nmax", [S, RING])
            prob = sba("prob", [S, RING, SK])
            pT = sba("pT", [KP, PR, KT * S])
            sums = sba("sums", [P, HEADS // 4 * S])
            rsum = sba("rsum", [S, HEADS])
            att = sba("att", [S, D])
            attT = sba("attT", [P, DK, S])
            prj = sba("prj", [S, D])

            def one_of(t, b):
                return t[bass.ds(b, 1), :, :].rearrange("o a b -> (o a) b")

            @block.sync
            def _(sp):
                sp.dma_start(x_sb[:], x.rearrange("b s d -> s b d")).then_inc(x_in, 16)

                def load_context(b, par):
                    sp.dma_start(ctx_sb[:, par], one_of(ctx, b).rearrange("(t p) d -> p t d", p=KP)).then_inc(ctx_in[par], 16)

                def load_mask(b, par):
                    sp.dma_start(mask_sb[:, par], one_of(mask.rearrange("b o s k -> (b o) s k"), b)).then_inc(mask_in[par], 16)

                for b in range(2):
                    load_context(b, b)
                    load_mask(b, b)
                sp.dma_start(wo_raw[:], wo_w.rearrange("(t p) d -> p t d", p=P)).then_inc(const_in, 16)
                sp.dma_start(wob[:], wo_b.rearrange("(o d) -> o d", o=1).to_broadcast([S, D])).then_inc(const_in, 16)
                sp.dma_start(gw_sb[:], gw.rearrange("(t p) e -> p t e", p=P)).then_inc(const_in, 16)
                sp.dma_start(gb_sb[:], gb.rearrange("(o d) -> o d", o=1).to_broadcast([S, E])).then_inc(const_in, 16)
                sp.dma_start(b1r[0:E, :], b1).then_inc(const_in, 16)
                sp.dma_start(b1r[E:NE, :], sb1.rearrange("(t p) -> t p", p=P)).then_inc(const_in, 16)
                sp.dma_start(b3r[0:E, :], b3).then_inc(const_in, 16)
                sp.dma_start(b3r[E:NE, :], sb3.rearrange("(t p) -> t p", p=P)).then_inc(const_in, 16)
                sp.wait_ge(b2_zero, 1)
                sp.dma_start(b2a[0:E, :], b2).then_inc(const_in, 16)
                sp.dma_start(b2a[E:E + 1, :], sb2.rearrange("(o d) -> o d", o=1)).then_inc(const_in, 16)
                load_expert(sp, 0, w1[0], w3[0], w2[0])
                load_expert(sp, 1, w1[1], w3[1], w2[1])
                with sp.Fori(1, B // 2) as i:
                    for par in range(2):
                        sp.wait_ge(stacked, 4 * (2 * i + par - 1))
                        sp.wait_ge(values_ok, 2 * i + par - 1)
                        load_context(2 * i + par, par)
                        sp.wait_ge(masked, NH * i - HEADS * (1 - par))
                        load_mask(2 * i + par, par)

            @block.gpsimd
            def _(pool):
                pool.memset(ident[:], 0.0).then_inc(ident_zero, 1)
                pool.wait_ge(ident_zero, 1)
                pool.affine_select(out=ident[:], in_=ident[:], compare_op=ALU.not_equal, fill=1.0, base=0,
                                   pattern=[[-1, P]], channel_multiplier=1).then_inc(ident_ok, 1)
                pool.memset(b2a[:], 0.0).then_inc(b2_zero, 1)
                pool.memset(kT[:, :, :, SK:SKE].bitcast(F32), 0.0).then_inc(kT_zero, 1)
                pool.wait_ge(ident_ok, 1)
                pool.tensor_copy(identr[:], ident[:]).then_inc(identr_ok, 1)
                pool.memset(vaug[:], 0.0).then_inc(values_zero, 1)
                pool.wait_ge(values_zero, 1)
                pool.memset(vaug[:, :, :, :, DH:DH + 1].rearrange("p a t h c -> p (a t h) c"), 1.0).then_inc(ones_ok, 1)
                pool.wait_ge(ones_ok, 1)

                def pair(i, first):
                    for par in range(2):
                        b = 2 * i + par
                        kin = ctx_sb[:, par].rearrange("p t (h c) -> p (t h) c", c=DH)
                        kview = kst[0:KP, par].rearrange("p t h f c -> p (t h) f c")
                        qin = q_sb[:, bass.ds(b, 1), :].rearrange("s o (h c) -> s (o h) c", c=DH)
                        qview = qst[:, par]
                        both = ((ctx_in[par], 16 * i + 16), (scores, HEADS * (b - 2) + 1))
                        waits_apart(pool, *both[:1 if first else 2])
                        for f in (0, 2):
                            pool.tensor_copy(kview[:, :, f, :], kin).then_inc(pool_hi, 1)
                        if first and par == 0:
                            pool.wait_ge(q_ok, 1)
                        for f in (0, 1):
                            pool.tensor_copy(qview[:, :, f, :], qin).then_inc(pool_hi, 1)
                        waits_apart(pool, (pool_hi, 4 * b + 4))
                        for f in (2, 3):
                            pool.tensor_tensor(qview[:, :, f, :], qin, qview[:, :, 0, :].bitcast(F32),
                                               ALU.subtract).then_inc(stacked, 1)
                        for f in (1, 3):
                            pool.tensor_tensor(kview[:, :, f, :], kin, kview[:, :, 0, :].bitcast(F32),
                                               ALU.subtract).then_inc(stacked, 1)
                        if not first:
                            waits_apart(pool, (pv_done, HEADS * (b - 1)))
                        pool.tensor_copy(vaug[:, par, :, :, 0:DH],
                                         ctx_sb[:, par].rearrange("p t (h c) -> p t h c", c=DH)
                                         ).then_inc(values_ok, 1)

                pool.wait_ge(kst_zero, 1)
                pair(0, True)
                with pool.Fori(1, B // 2) as i:
                    pair(i, False)

            def prep_fill(pe, n, b, par, bank):
                auxr = ps[:, AUX + bank, :].bitcast(F32R)
                if n == 0:
                    pe.wait_ge(stacked, 4 * b + 4)
                if n < NQU:
                    for g in range(4):
                        h2 = n * 4 + g
                        last = nc.tensor.transpose(auxr[:, g * S:(g + 1) * S],
                                                   qst[:, par, 2 * h2:2 * h2 + 2].rearrange("s h f c -> s (h f c)"),
                                                   identr[0:S, 0:S])
                else:
                    g = n - NQU
                    for t in range(KT):
                        last = nc.tensor.transpose(auxr[:, t * KPE:(t + 1) * KPE],
                                                   kst[:, par, t, 2 * g:2 * g + 2].rearrange("s h f c -> s (h f c)"),
                                                   identr[0:KPE, 0:KPE])
                last.then_inc(aux_full, 1)

            def prep_read(n, par, bank):
                auxb = ps[:, AUX + bank, :]
                if n < NQU:
                    return (qT[:, par, 4 * n:4 * n + 4, :].rearrange("p g s -> p (g s)"), auxb[:, 0:4 * S])
                return (kT[:, par, n - NQU, 0:SK].rearrange("p (t k) -> p t k", t=KT),
                        auxb[:, 0:KT * KPE].rearrange("p (t k) -> p t k", t=KT)[:, :, 0:KP])

            @block.tensor
            def _(pe):
                pe.wait_ge(ident_ok, 1)
                pe.wait_ge(identr_ok, 1)
                pe.wait_ge(const_in, 16 * 10)
                for t in range(DK):
                    for k in range(DK):
                        nc.tensor.transpose(ps[:, 0, (k * DK + t) * P:(k * DK + t + 1) * P],
                                            wo_raw[:, t, k * P:(k + 1) * P], ident[:])
                nc.tensor.transpose(ps[:, 1, 0:NE], b1r[:], ident[0:NE, 0:NE])
                nc.tensor.transpose(ps[:, 1, P:P + NE], b3r[:], ident[0:NE, 0:NE]).then_inc(bias_T, 1)
                pe.wait_ge(bias_copied, 3)
                for n in range(NPREP):
                    if n >= 2:
                        pe.wait_ge(aux_by_act if n % 2 == 0 else aux_by_dve, n // 2)
                    prep_fill(pe, n, 0, 0, n % 2)

                def pair(i, first, last):
                    plan = aux_plan(first, last)

                    def unit(j):
                        _, kind, n, later, _ = plan[j]
                        bank = aux_bank(i, j)
                        auxb = ps[:, AUX + bank, :]
                        nd, na = aux_reads(i, plan, j if kind in ("ctxT", "proj") else j - 1)
                        pe.wait_ge(aux_by_dve, nd)
                        pe.wait_ge(aux_by_act, na)
                        if kind == "prep":
                            prep_fill(pe, n, 2 * i + later, later % 2, bank)
                            return
                        if kind == "turn":
                            pe.wait_ge(sums_ok, 2 * i + later + 1)
                            for g in range(HEADS // 4):
                                ins = nc.tensor.transpose(auxb[0:S, g * P:(g + 1) * P], sums[:, g * S:(g + 1) * S],
                                                          ident[:])
                        elif kind == "ctxT":
                            for k in range(DK):
                                ins = nc.tensor.transpose(auxb[:, k * S:(k + 1) * S], att[:, k * P:(k + 1) * P],
                                                          ident[0:S, 0:S])
                        else:
                            for k in range(DK):
                                ins = nc.tensor.matmul(auxb[0:S, 0:D], attT[:, k, :], woT[:, k, :],
                                                       start=(k == 0), stop=(k == DK - 1))
                        ins.then_inc(aux_full, 1)

                    j = 0
                    for n in range(NSTEPS if last else NH):
                        if n < NH:
                            half, h = n // HEADS, n % HEADS
                            r = 64 * (h % 2)
                            if h == 0:
                                done = [k for k, u in enumerate(plan) if u[1] == "prep" and u[3] == half]
                                nd, na = aux_reads(i, plan, done[-1] + 1 if done else 0)
                                pe.wait_ge(aux_by_dve, nd)
                                pe.wait_ge(aux_by_act, na)
                            wait(pe, masked, NH * i + n - SR + 1)
                            nc.tensor.matmul(ps[0:S, n % SR, 0:SKE], qT[r:r + 64, half, h // 2, :],
                                             kT[r:r + 64, half, h // 2, :], start=True, stop=True).then_inc(scores, 1)
                        d = n - T_LAG
                        if (d >= 0 or not first) and d < NH:
                            pe.wait_ge(exped, NH * i + d + 1)
                            nd, na = copies(d - TR + 1)
                            wait(pe, pT_by_dve, D_PAIR * i + nd)
                            wait(pe, pT_by_act, A_PAIR * i + na)
                            for t in range(KT):
                                ins = nc.tensor.transpose(ps[0:KP, PT_BANK + d % TR, t * S:(t + 1) * S],
                                                          prob[:, d % RING, t * KP:(t + 1) * KP], ident[0:S, 0:S])
                            ins.then_inc(p_turned, 1)
                        d = n - PV_LAG
                        if (d >= 0 or not first) and d < NH:
                            nd, na = copies(d + 1)
                            wait(pe, pT_by_dve, D_PAIR * i + nd)
                            wait(pe, pT_by_act, A_PAIR * i + na)
                            h = d % HEADS
                            if h == 0:
                                wait(pe, sums_ok, 2 * i + d // HEADS - 1)
                                pe.wait_ge(values_ok, 2 * i + d // HEADS + 1)
                            row = VC * (h % 4)
                            for t in range(KT):
                                ins = nc.tensor.matmul(ps[row:row + VC, SUM_BANK + (d // HEADS) % 2, h // 4 * S:(h // 4 + 1) * S],
                                                       vaug[:, (d // HEADS) % 2, t, h, :],
                                                       pT[:, d % PR, t * S:(t + 1) * S],
                                                       start=(t == 0), stop=(t == KT - 1))
                            ins.then_inc(pv_done, 1)
                        while j < len(plan) and plan[j][0] == n:
                            unit(j)
                            j += 1
                    assert j == len(plan)

                pair(0, True, False)
                with pe.Fori(1, B // 2 - 1) as i:
                    pair(i, False, False)
                pair(B // 2 - 1, False, True)

            @block.scalar
            def _(act):
                act.wait_ge(var_ok, 1)
                nc.scalar.activation(std[:], veps[:], ACT.Sqrt).then_inc(std_ok, 1)
                act.wait_ge(bias_T, 1)
                nc.scalar.copy(b1T[:], ps[:, 1, 0:NE]).then_inc(bias_copied, 1)
                nc.scalar.copy(b3T[:], ps[:, 1, P:P + NE]).then_inc(bias_copied, 1)

                def read_prep(n, par, bank):
                    dst, src = prep_read(n, par, bank)
                    nc.scalar.copy(dst, src).then_inc(aux_by_act, 1)

                act.wait_ge(kT_zero, 1)
                for n in range(NPREP):
                    if n % 2 == 0:
                        act.wait_ge(aux_full, n + 1)
                        read_prep(n, 0, n % 2)

                def pair(i, first, last):
                    plan = aux_plan(first, last)
                    j = 0
                    for n in range(NSTEPS if last else NH):
                        d = n - C_LAG
                        if (d >= 0 or not first) and d < NH and not copied_by_dve(d):
                            act.wait_ge(p_turned, NH * i + d + 1)
                            wait(act, pv_done, NH * i + d - PR + 1)
                            nc.scalar.copy(pT[:, d % PR, :], ps[0:KP, PT_BANK + d % TR, 0:KT * S]).then_inc(pT_by_act, 1)
                        if n < NH:
                            act.wait_ge(masked, NH * i + n + 1)
                            wait(act, p_turned, NH * i + n - RING + 1)
                            nc.scalar.activation(prob[:, n % RING, :], nsm[:, n % RING, :], ACT.Exp, scale=-1.0,
                                                 bias=nmax[:, n % RING:n % RING + 1]).then_inc(exped, 1)
                        for ends in (0, HEADS, NH):
                            if n == ends + DRAIN_AT and not (first and ends == 0):
                                act.wait_ge(pv_done, NH * i + ends)
                                nc.scalar.copy(sums[:], ps[:, SUM_BANK + (ends // HEADS + 1) % 2, 0:HEADS // 4 * S]).then_inc(sums_ok, 1)
                        while j < len(plan) and plan[j][0] == n:
                            _, kind, k, later, who = plan[j]
                            if who == "ACT":
                                act.wait_ge(aux_full, aux_base(i) + j + 1)
                                if kind == "prep":
                                    read_prep(k, later % 2, aux_bank(i, j))
                                else:
                                    nc.scalar.copy(attT[:].rearrange("p k s -> p (k s)"),
                                                   ps[:, AUX + aux_bank(i, j), 0:DK * S]).then_inc(aux_by_act, 1)
                            j += 1

                pair(0, True, False)
                with act.Fori(1, B // 2 - 1) as i:
                    pair(i, False, False)
                pair(B // 2 - 1, False, True)

            @block.vector
            def _(dve):
                nc.vector.memset(kst[96:KPE].bitcast(F32), 0.0).then_inc(kst_zero, 1)
                dve.wait_ge(x_in, 16)
                for b in range(B):
                    nc.vector.bn_stats(stats[:, b, :], x_sb[:, b, :]).then_inc(dve_step, 1)
                dve.wait_ge(dve_step, B)
                for b in range(B):
                    nc.vector.bn_aggr(mv[:, b, :], stats[:, b, :]).then_inc(dve_step, 1)
                dve.wait_ge(dve_step, 2 * B)
                nc.vector.tensor_scalar(veps[:], mv[:, :, 1], EPS, None, ALU.add).then_inc(var_ok, 1)
                dve.wait_ge(std_ok, 1)
                nc.vector.reciprocal(rstd[:], std[:]).then_inc(dve_step, 1)
                dve.wait_ge(dve_step, 2 * B + 1)
                for b in range(B):
                    ins = nc.vector.tensor_scalar(q_sb[:, b, :], x_sb[:, b, :], mv[:, b, 0:1], rstd[:, b:b + 1],
                                                  ALU.subtract, ALU.mult)
                ins.then_inc(q_ok, 1)
                dve.wait_ge(bias_T, 1)
                nc.vector.tensor_copy(woT[:].rearrange("p k d -> p (k d)"), ps[:, 0, :]).then_inc(bias_copied, 1)

                def read_prep(n, par, bank):
                    dst, src = prep_read(n, par, bank)
                    nc.vector.tensor_copy(dst, src).then_inc(aux_by_dve, 1)

                dve.wait_ge(kT_zero, 1)
                for n in range(NPREP):
                    if n % 2 == 1:
                        dve.wait_ge(aux_full, n + 1)
                        read_prep(n, 0, n % 2)

                def pair(i, first, last):
                    plan = aux_plan(first, last)
                    j = 0
                    for n in range(NSTEPS if last else NH):
                        d = n - C_LAG
                        if (d >= 0 or not first) and d < NH and copied_by_dve(d):
                            dve.wait_ge(p_turned, NH * i + d + 1)
                            wait(dve, pv_done, NH * i + d - PR + 1)
                            nc.vector.tensor_copy(pT[:, d % PR, :], ps[0:KP, PT_BANK + d % TR, 0:KT * S]
                                                  ).then_inc(pT_by_dve, 1)
                        if n < NH:
                            half = n // HEADS
                            if n % HEADS == 0:
                                dve.wait_ge(mask_in[half], 16 * i + 16)
                            two = [(scores, NH * i + n + 1), (exped, NH * i + n - RING + 1)]
                            if first:
                                for q, v in two:
                                    wait(dve, q, v)
                            else:
                                waits_apart(dve, *two)
                            nc.vector.tensor_tensor_reduce(
                                out=nsm[:, n % RING, :], in0=ps[0:S, n % SR, 0:SK], in1=mask_sb[:, half, :],
                                scale=-1.0, scalar=BIG, op0=ALU.add, op1=ALU.min,
                                accum_out=nmax[:, n % RING:n % RING + 1]).then_inc(masked, 1)
                        while j < len(plan) and plan[j][0] == n:
                            _, kind, k, later, who = plan[j]
                            b = 2 * i + later
                            auxb = ps[:, AUX + aux_bank(i, j), :]
                            if who == "DVE":
                                dve.wait_ge(aux_full, aux_base(i) + j + 1)
                            if kind == "prep" and who == "DVE":
                                read_prep(k, later % 2, aux_bank(i, j))
                            elif kind == "turn":
                                heads = auxb[0:S, :].rearrange("s (h c) -> s h c", c=VC)
                                nc.vector.reciprocal(rsum[:], heads[:, :, DH]).then_inc(rsum_ok, 1)
                                dve.wait_ge(rsum_ok, b + 1)
                                nc.vector.tensor_tensor(att[:].rearrange("s (h c) -> s h c", c=DH), heads[:, :, 0:DH],
                                                        rsum[:].unsqueeze(2).to_broadcast([S, HEADS, DH]),
                                                        ALU.mult).then_inc(aux_by_dve, 1)
                            elif kind == "proj":
                                xb = x_sb[:, bass.ds(b, 1), :].rearrange("s o d -> s (o d)")
                                x2b = x2[:, bass.ds(b, 1), :].rearrange("s o d -> s (o d)")
                                nc.vector.tensor_tensor(prj[:], auxb[0:S, 0:D], wob[:], ALU.add).then_inc(aux_by_dve, 1)
                                dve.wait_ge(aux_by_dve, aux_reads(i, plan, j + 1)[0])
                                nc.vector.scalar_tensor_tensor(x2b, prj[:], 0.0, xb, ALU.max, ALU.add).then_inc(x2_ok, 1)
                                dve.wait_ge(x2_ok, b + 1)
                                nc.vector.bn_stats(stats[:, bass.ds(b, 1), :].rearrange("s o d -> s (o d)"), x2b)
                            j += 1

                pair(0, True, False)
                with dve.Fori(1, B // 2 - 1) as i:
                    pair(i, False, False)
                pair(B // 2 - 1, False, True)

        w_in = [sem("w_in0"), sem("w_in1")]
        gate_in = [sem("gate_in0"), sem("gate_in1")]
        gate_out = sem("gate_out")
        xn_ok = sem("xn_ok")
        xT_full = sem("xT_full")
        xf_ok = sem("xf_ok")
        xhi_ok = sem("xhi_ok")
        xlo_ok = sem("xlo_ok")
        logits_ok = sem("logits_ok")
        lmax_ok = sem("lmax_ok")
        probs_ok = sem("probs_ok")
        cw_ok = sem("cw_ok")
        cw_turned = sem("cw_turned")
        cwT_ok = sem("cwT_ok")
        const_ok = sem("const_ok")
        whi_up = sem("whi_up")
        wlo_up = sem("wlo_up")
        whi_down = sem("whi_down")
        wlo_down = sem("wlo_down")
        h1_full = sem("h1_full")
        h3_full = sem("h3_full")
        silu_ok = sem("silu_ok")
        gated = sem("gated")
        h_ok = sem("h_ok")
        hhi_ok = sem("hhi_ok")
        hlo_ok = sem("hlo_ok")
        down_done = sem("down_done")
        y_by_act = sem("y_by_act")
        y_by_dve = sem("y_by_dve")
        y_turned = sem("y_turned")
        out_ok = sem("out_ok")
        out_sent = sem("out_sent")
        std2_ok = sem("std2_ok")
        var2_ok = sem("var2_ok")

        def load_expert(sp, slot, a1, a3, a2):
            sp.dma_start(wr[:, slot, 0:DK, 0:INTER], a1.rearrange("(k p) i -> p k i", p=P)).then_inc(w_in[slot], 16)
            sp.dma_start(wr[:, slot, 0:DK, INTER:D], a3.rearrange("(k p) i -> p k i", p=P)).then_inc(w_in[slot], 16)
            sp.dma_start(wr[:, slot, DK, :], a2).then_inc(w_in[slot], 16)

        def experts(block, sbe):
            xn = sbe("xn", [S, B, D])
            xf = sbe("xf", [P, DK, T])
            xhi = sbe("xhi", [P, DK, T], F32R)
            xlo = sbe("xlo", [P, DK, T], F32R)
            whi = sbe("whi", [P, 2, 3, D], F32R)
            wlo = sbe("wlo", [P, 2, 3, D], F32R)
            lg = sbe("lg", [S, B, E])
            lmax = sbe("lmax", [S, B])
            ld = sbe("ld", [S, B, E])
            ex = sbe("ex", [S, B, E])
            esum = sbe("esum", [S, B])
            sc = sbe("sc", [S, B, E])
            pmax = sbe("pmax", [S, B * GROUPS, 2])
            pmin = sbe("pmin", [S, B * GROUPS, 2])
            top1 = sbe("top1", [S, B * GROUPS])
            lowm = sbe("lowm", [S, B * GROUPS])
            highm = sbe("highm", [S, B * GROUPS])
            top2 = sbe("top2", [S, B * GROUPS])
            gs = sbe("gs", [S, B, GROUPS])
            keep = sbe("keep", [S, B, GROUPS])
            keepm = sbe("keepm", [S, B, GROUPS])
            msc = sbe("msc", [S, B, E])
            sel = sbe("sel", [S, B, E])
            best = sbe("best", [S, B, 8])
            above = sbe("above", [S, B, E])
            equal = sbe("equal", [S, B, E])
            naabove = sbe("naabove", [S, B])
            prefix = sbe("prefix", [S, B, E])
            restart = sbe("restart", [S, B, E])
            restart_g = sbe("restart_g", [S, B, GROUPS])
            cw = sbe("cw", [S, B, NE])
            cwT = sbe("cwT", [NE, T])
            we = sbe("we", [P, 2, T])
            sil = sbe("sil", [P, 2, CT])
            tg = sbe("tg", [P, 2, CT])
            hf = sbe("hf", [P, 2, CT])
            hhi = sbe("hhi", [P, 2, CT], F32R)
            hlo = sbe("hlo", [P, 2, CT], F32R)
            yT = sbe("yT", [P, DK, T])
            o_sb = sbe("o_sb", [S, B, D])

            def up_ps(which, par):
                return ps[:, 2 * par + which, 0:CT]

            def y_ps(k, c):
                return ps[:, 4 + 2 * k + c, 0:CT]

            NU = 2 * NE
            NPAIR = NE // 2

            @block.sync
            def _(sp):
                def gate_row(e, slot):
                    sp.dma_start(we[:, slot, :], scratch[bass.ds(e, 1), :].to_broadcast([P, T])).then_inc(gate_in[slot], 16)

                for c in range(NCH):
                    sp.wait_ge(cwT_ok, c + 1)
                    sp.dma_start(scratch[:, c * CT:(c + 1) * CT], cwT[:, c * CT:(c + 1) * CT]).then_inc(gate_out, 16)
                sp.wait_ge(gate_out, 16 * NCH)
                gate_row(0, 0)
                gate_row(1, 1)

                def refill(e, slot, shared):
                    for q in (whi_up, wlo_up, whi_down, wlo_down):
                        sp.wait_ge(q, e - 1)
                    if shared:
                        cols = slice(slot * INTER, (slot + 1) * INTER)
                        load_expert(sp, slot, sw1[:, cols], sw3[:, cols], sw2[cols, :])
                    else:
                        load_expert(sp, slot, one(w1, e), one(w3, e), one(w2, e))
                    sp.wait_ge(gated, 2 * (e - 1))
                    gate_row(e, slot)

                def one(w, e):
                    return w[bass.ds(e, 1), :, :].rearrange("o a b -> (o a) b")

                with sp.Fori(1, NPAIR - 1) as i:
                    for slot in range(2):
                        refill(2 * i + slot, slot, False)
                for slot in range(2):
                    refill(E + slot, slot, True)

                for q in range(B // 2):
                    sp.wait_ge(out_ok, 2 * q + 2)
                    sp.dma_start(out[2 * q:2 * q + 2].rearrange("b s d -> s b d"),
                                 o_sb[:, 2 * q:2 * q + 2, :]).then_inc(out_sent, 16)
                sp.wait_ge(out_sent, 16 * (B // 2))

            @block.gpsimd
            def _(pool):
                pool.memset(restart[:], 1.0).then_inc(const_ok, 1)
                pool.memset(restart_g[:], 1.0).then_inc(const_ok, 1)
                pool.memset(cw[:], 1.0).then_inc(const_ok, 1)
                pool.wait_ge(const_ok, 3)
                pool.memset(restart[:, :, 0:1], 0.0).then_inc(const_ok, 1)
                pool.memset(restart_g[:, :, 0:1], 0.0).then_inc(const_ok, 1)

            @block.tensor
            def _(pe):
                pe.wait_ge(xn_ok, 1)
                for c in range(NCH):
                    for k in range(DK):
                        for b in range(CB):
                            ins = nc.tensor.transpose(ps[:, 2 * c + k, b * S:(b + 1) * S],
                                                      xn[:, c * CB + b, k * P:(k + 1) * P], ident[0:S, 0:S])
                        ins.then_inc(xT_full, 1)
                pe.wait_ge(xf_ok, 2 * NCH)
                for b in range(B):
                    for k in range(DK):
                        ins = nc.tensor.matmul(ps[0:S, 4, b * E:(b + 1) * E], xf[:, k, b * S:(b + 1) * S],
                                               gw_sb[:, k, :], start=(k == 0), stop=(k == DK - 1))
                ins.then_inc(logits_ok, 1)

                pe.wait_ge(xhi_ok, 2 * NCH)
                pe.wait_ge(xlo_ok, 2 * NCH)

                def up(u, e, slot, c):
                    if c == 0:
                        pe.wait_ge(whi_up, e + 1)
                        pe.wait_ge(wlo_up, e + 1)
                    par = c
                    for which, full, read in ((0, h1_full, silu_ok), (1, h3_full, h_ok)):
                        if u is not None:
                            pe.wait_ge(read, u - 1)
                        n = 0
                        cols = slice(which * INTER, (which + 1) * INTER)
                        for k in range(DK):
                            toks = slice(c * CT, (c + 1) * CT)
                            for wt, xt in ((whi, xhi), (whi, xlo), (wlo, xhi)):
                                ins = nc.tensor.matmul(up_ps(which, par), wt[:, slot, k, cols], xt[:, k, toks],
                                                       start=(n == 0), stop=(n == 3 * DK - 1))
                                n += 1
                        ins.then_inc(full, 1)

                def down(u, e, slot, c, last=False):
                    if c == 0:
                        pe.wait_ge(whi_down, e + 1)
                        pe.wait_ge(wlo_down, e + 1)
                    pe.wait_ge(hhi_ok, u + 1)
                    order = [(whi, hhi, k) for k in range(DK)] + [(wlo, hhi, k) for k in range(DK)]
                    order += [(whi, hlo, k) for k in range(DK)]
                    for n, (wt, ht, k) in enumerate(order):
                        if n == 2 * DK:
                            pe.wait_ge(hlo_ok, u + 1)
                        ins = nc.tensor.matmul(y_ps(k, c), wt[:, slot, DK, k * P:(k + 1) * P], ht[:, c, :],
                                               start=False, stop=last and n >= 2 * DK, skip_group_check=True)
                    ins.then_inc(down_done, 1)

                up(None, 0, 0, 0)
                pe.wait_ge(cw_ok, 1)
                for c in range(NCH):
                    for b in range(CB):
                        ins = nc.tensor.transpose(ps[0:NE, 2 + c, b * S:(b + 1) * S], cw[:, c * CB + b, :],
                                                  ident[0:S, 0:S])
                    ins.then_inc(cw_turned, 1)
                pe.wait_ge(cwT_ok, NCH)
                for c in range(NCH):
                    for k in range(DK):
                        nc.tensor.matmul(y_ps(k, c), b2a[:, k * P:(k + 1) * P], cwT[:, c * CT:(c + 1) * CT],
                                         start=True, stop=False, skip_group_check=True)
                up(None, 0, 0, 1)
                down(0, 0, 0, 0)
                up(2, 1, 1, 0)
                down(1, 0, 0, 1)
                up(3, 1, 1, 1)
                down(2, 1, 1, 0)

                with pe.Fori(1, NPAIR) as i:
                    up(4 * i, 2 * i, 0, 0)
                    down(4 * i - 1, 2 * i - 1, 1, 1)
                    up(4 * i + 1, 2 * i, 0, 1)
                    down(4 * i, 2 * i, 0, 0)
                    up(4 * i + 2, 2 * i + 1, 1, 0)
                    down(4 * i + 1, 2 * i, 0, 1)
                    up(4 * i + 3, 2 * i + 1, 1, 1)
                    down(4 * i + 2, 2 * i + 1, 1, 0)
                down(NU - 1, NE - 1, 1, 1, True)

                for b in range(B):
                    c = b // CB
                    if b % CB == 0:
                        pe.wait_ge(y_by_act, c + 1)
                        pe.wait_ge(y_by_dve, c + 1)
                    for k in range(DK):
                        ins = nc.tensor.transpose(ps[0:S, b // 2, (b % 2) * D + k * P:(b % 2) * D + (k + 1) * P],
                                                  yT[:, k, b * S:(b + 1) * S], ident[:])
                    ins.then_inc(y_turned, 1)

            @block.scalar
            def _(act):
                act.wait_ge(var2_ok, 1)
                nc.scalar.activation(std[:], veps[:], ACT.Sqrt).then_inc(std2_ok, 1)
                for n in range(2 * NCH):
                    c, k = n // DK, n % DK
                    act.wait_ge(xT_full, n + 1)
                    nc.scalar.copy(xf[:, k, c * CT:(c + 1) * CT], ps[:, n, 0:CT]).then_inc(xf_ok, 1)
                    nc.scalar.copy(xhi[:, k, c * CT:(c + 1) * CT], ps[:, n, 0:CT]).then_inc(xhi_ok, 1)
                def split_hi_up(e, slot, n):
                    act.wait_ge(w_in[slot], 48 * (n + 1))
                    if e is not None:
                        act.wait_ge(h3_full, 2 * e - 2)
                        act.wait_ge(wlo_up, e - 1)
                    nc.scalar.copy(whi[:, slot, 0:DK].rearrange("p k d -> p (k d)"),
                                   wr[:, slot, 0:DK].rearrange("p k d -> p (k d)")).then_inc(whi_up, 1)

                def split_hi_down(e, slot):
                    if e is not None:
                        act.wait_ge(down_done, 2 * e - 2)
                        act.wait_ge(wlo_down, e - 1)
                    nc.scalar.copy(whi[:, slot, DK], wr[:, slot, DK]).then_inc(whi_down, 1)

                for slot in range(2):
                    split_hi_up(None, slot, 0)
                    split_hi_down(None, slot)
                act.wait_ge(lmax_ok, 1)
                nc.scalar.activation(ex[:], ld[:], ACT.Exp).then_inc(probs_ok, 1)

                def silu(u, e, c):
                    waits_apart(act, (h1_full, u + 1))
                    nc.scalar.activation(sil[:, c, :], up_ps(0, c), ACT.Silu,
                                         bias=b1T[:, bass.ds(e, 1)]).then_inc(silu_ok, 1)

                def hi(u, c):
                    act.wait_ge(h_ok, u + 1)
                    nc.scalar.copy(hhi[:, c, :], hf[:, c, :]).then_inc(hhi_ok, 1)


                def pair(i, last, first=False):
                    for s in range(2):
                        e = 2 * i + s
                        for c in range(2):
                            u = 2 * e + c
                            silu(u, e, c)
                            if not (s == 0 and first) and not (last and s == 1):
                                if c == 0:
                                    split_hi_up(e + 1, 1 - s, i + s)
                                else:
                                    split_hi_down(e + 1, 1 - s)
                            hi(u, c)

                pair(0, False, True)
                with act.Fori(1, NPAIR - 1) as i:
                    pair(i, False)
                pair(NPAIR - 1, True)
                for n in range(2 * NCH):
                    c, k = n // DK, n % DK
                    if n % 2 == 0:
                        act.wait_ge(down_done, NU - 1 + c)
                        nc.scalar.copy(yT[:, k, c * CT:(c + 1) * CT], y_ps(k, c)).then_inc(y_by_act, 1)

            @block.vector
            def _(dve):
                steps = {"n": 0}

                def chained(ins):
                    steps["n"] += 1
                    ins.then_inc(gate_step, 1)
                    dve.wait_ge(gate_step, steps["n"])

                gate_step = dve_step2
                TT = nc.vector.tensor_tensor
                for b in range(B):
                    ins = nc.vector.bn_aggr(mv[:, b, :], stats[:, b, :])
                chained(ins)
                nc.vector.tensor_scalar(veps[:], mv[:, :, 1], EPS, None, ALU.add).then_inc(var2_ok, 1)
                dve.wait_ge(std2_ok, 1)
                chained(nc.vector.reciprocal(rstd[:], std[:]))
                for b in range(B):
                    ins = nc.vector.tensor_scalar(xn[:, b, :], x2[:, b, :], mv[:, b, 0:1], rstd[:, b:b + 1],
                                                  ALU.subtract, ALU.mult)
                ins.then_inc(xn_ok, 1)
                for n in range(2 * NCH):
                    c, k = n // DK, n % DK
                    toks = slice(c * CT, (c + 1) * CT)
                    dve.wait_ge(xf_ok, n + 1)
                    dve.wait_ge(xhi_ok, n + 1)
                    TT(xlo[:, k, toks], xf[:, k, toks], xhi[:, k, toks].bitcast(F32), ALU.subtract).then_inc(xlo_ok, 1)

                def split_lo(e, slot, ks, hi_made, lo_made):
                    dve.wait_ge(hi_made, e + 1)
                    TT(wlo[:, slot, ks].rearrange("p k d -> p (k d)"), wr[:, slot, ks].rearrange("p k d -> p (k d)"),
                       whi[:, slot, ks].rearrange("p k d -> p (k d)").bitcast(F32), ALU.subtract).then_inc(lo_made, 1)

                def split_lo_up(e, slot):
                    split_lo(e, slot, slice(0, DK), whi_up, wlo_up)

                def split_lo_down(e, slot):
                    split_lo(e, slot, slice(DK, DK + 1), whi_down, wlo_down)

                def over(ap, shape):
                    return ap.unsqueeze(2).to_broadcast(shape)

                for slot in range(2):
                    split_lo_up(slot, slot)
                    split_lo_down(slot, slot)
                dve.wait_ge(logits_ok, 1)
                chained(TT(lg[:], ps[0:S, 4, 0:B * E].rearrange("s (b e) -> s b e", e=E),
                           gb_sb[:].unsqueeze(1).to_broadcast([S, B, E]), ALU.add))
                chained(nc.vector.tensor_reduce(lmax[:], lg[:], AX.X, ALU.max))
                TT(ld[:], lg[:], over(lmax[:], [S, B, E]), ALU.subtract).then_inc(lmax_ok, 1)
                dve.wait_ge(probs_ok, 1)
                chained(nc.vector.tensor_reduce(esum[:], ex[:], AX.X, ALU.add))
                chained(nc.vector.reciprocal(lmax[:], esum[:]))
                chained(TT(sc[:], ex[:], over(lmax[:], [S, B, E]), ALU.mult))
                four = sc[:].rearrange("s b (g f) -> s (b g) f", f=GE)
                nc.vector.tensor_tensor(pmax[:], four[:, :, 0:2], four[:, :, 2:4], ALU.max)
                chained(TT(pmin[:], four[:, :, 0:2], four[:, :, 2:4], ALU.min))
                TT(top1[:], pmax[:, :, 0], pmax[:, :, 1], ALU.max)
                TT(lowm[:], pmax[:, :, 0], pmax[:, :, 1], ALU.min)
                chained(TT(highm[:], pmin[:, :, 0], pmin[:, :, 1], ALU.max))
                chained(TT(top2[:], lowm[:], highm[:], ALU.max))
                chained(TT(gs[:].rearrange("s b g -> s (b g)"), top1[:], top2[:], ALU.add))

                def choose(chosen, values, width, count, starts):
                    for b in range(B):
                        ins = nc.vector.max(best[:, b, :], values[:, b, :])
                    chained(ins)
                    lim = best[:, :, count - 1:count].to_broadcast([S, B, width])
                    ab, eq, pf = above[:, :, 0:width], equal[:, :, 0:width], prefix
                    if width != E:
                        ab = above[:].rearrange("s b e -> s (b e)")[:, 0:B * width].rearrange("s (b w) -> s b w", w=width)
                        eq = equal[:].rearrange("s b e -> s (b e)")[:, 0:B * width].rearrange("s (b w) -> s b w", w=width)
                    pf = prefix[:].rearrange("s b e -> s (b e)")[:, 0:B * width]
                    TT(ab, values, lim, ALU.is_gt)
                    chained(TT(eq, values, lim, ALU.is_equal))
                    nc.vector.tensor_reduce(naabove[:], ab, AX.X, ALU.add)
                    chained(nc.vector.tensor_tensor_scan(pf, starts[:].rearrange("s b w -> s (b w)"),
                                                         eq.rearrange("s b w -> s (b w)"), 0.0, ALU.mult, ALU.add))
                    pf3 = pf.rearrange("s (b w) -> s b w", w=width)
                    chained(TT(pf3, pf3, over(naabove[:], [S, B, width]), ALU.add))
                    chained(nc.vector.scalar_tensor_tensor(eq, pf3, float(count), eq, ALU.is_le, ALU.mult))
                    chained(TT(chosen, ab, eq, ALU.add))

                dve.wait_ge(const_ok, 5)
                choose(keep[:], gs[:], GROUPS, KEEP_GROUPS, restart_g)
                chained(nc.vector.tensor_scalar(keepm[:], keep[:], -1.0, None, ALU.add))
                k4 = keep[:].rearrange("s b g -> s (b g)").unsqueeze(2).to_broadcast([S, B * GROUPS, GE])
                km4 = keepm[:].rearrange("s b g -> s (b g)").unsqueeze(2).to_broadcast([S, B * GROUPS, GE])
                m4 = msc[:].rearrange("s b (g f) -> s (b g) f", f=GE)
                chained(TT(m4, four, k4, ALU.mult))
                chained(TT(m4, m4, km4, ALU.add))
                choose(sel[:], msc[:], E, TOPK, restart)
                TT(cw[:, :, 0:E], sc[:], sel[:], ALU.mult).then_inc(cw_ok, 1)
                for c in range(NCH):
                    dve.wait_ge(cw_turned, c + 1)
                    nc.vector.tensor_copy(cwT[:, c * CT:(c + 1) * CT], ps[0:NE, 2 + c, 0:CT]).then_inc(cwT_ok, 1)

                def unit_gate(u, slot, c, n):
                    dve.wait_ge(silu_ok, u + 1)
                    dve.wait_ge(gate_in[slot], 16 * (n + 1))
                    TT(tg[:, c, :], sil[:, c, :], we[:, slot, c * CT:(c + 1) * CT], ALU.mult).then_inc(gated, 1)

                def unit_h(u, e, c):
                    dve.wait_ge(h3_full, u + 1)
                    dve.wait_ge(gated, u + 1)
                    nc.vector.scalar_tensor_tensor(hf[:, c, :], up_ps(1, c), b3T[:, bass.ds(e, 1)], tg[:, c, :],
                                                   ALU.add, ALU.mult).then_inc(h_ok, 1)

                def unit_lo(u, c):
                    dve.wait_ge(hhi_ok, u + 1)
                    TT(hlo[:, c, :], hf[:, c, :], hhi[:, c, :].bitcast(F32), ALU.subtract).then_inc(hlo_ok, 1)

                def pair(i, last, first=False):
                    for s in range(2):
                        e = 2 * i + s
                        for c in range(2):
                            u = 2 * e + c
                            unit_gate(u, s, c, i)
                            unit_h(u, e, c)
                            if not (s == 0 and first) and not (last and s == 1):
                                if c == 0:
                                    split_lo_up(e + 1, 1 - s)
                                else:
                                    split_lo_down(e + 1, 1 - s)
                            unit_lo(u, c)

                pair(0, False, True)
                with dve.Fori(1, NPAIR - 1) as i:
                    pair(i, False)
                pair(NPAIR - 1, True)
                for n in range(2 * NCH):
                    c, k = n // DK, n % DK
                    if n % 2 == 1:
                        dve.wait_ge(down_done, NU - 1 + c)
                        nc.vector.tensor_copy(yT[:, k, c * CT:(c + 1) * CT], y_ps(k, c)).then_inc(y_by_dve, 1)
                for b in range(B):
                    dve.wait_ge(y_turned, 2 * (b // 2) + 2)
                    TT(o_sb[:, b, :], ps[0:S, b // 2, (b % 2) * D:(b % 2 + 1) * D], x2[:, b, :], ALU.add).then_inc(out_ok, 1)

        with ExitStack() as own:
            attention(own.enter_context(nc.Block()), lambda n, s, d=F32: own.enter_context(nc.sbuf_tensor(n, s, d)))
        with ExitStack() as own:
            experts(own.enter_context(nc.Block()), lambda n, s, d=F32: own.enter_context(nc.sbuf_tensor(n, s, d)))


_INS = ["x", "ctx_1024", "mask_Bx1xSxS2_ff0", "L0_xattn_wo_w", "L0_xattn_wo_b", "L0_ffn_gw", "L0_ffn_gb",
        "L0_ffn_w1", "L0_ffn_b1", "L0_ffn_w3", "L0_ffn_b3", "L0_ffn_w2", "L0_ffn_b2", "L0_ffn_sw1",
        "L0_ffn_sb1", "L0_ffn_sw3", "L0_ffn_sb3", "L0_ffn_sw2", "L0_ffn_sb2"]


def kernel(**inputs):
    import numpy as _np
    import concourse.bacc as _bacc
    from concourse import mybir as _mybir
    from concourse.bass_utils import run_bass_kernel_spmd as _run

    nc = _bacc.Bacc("TRN2", target_bir_lowering=False, num_devices=1)
    arrays, args = {}, []
    for name in _INS:
        a = _np.ascontiguousarray(inputs[name])
        arrays[f"in_{name}"] = a
        args.append(nc.dram_tensor(f"in_{name}", a.shape, _mybir.dt.from_np(a.dtype), kind="ExternalInput").ap())
    shape = inputs["x"].shape
    args.append(nc.dram_tensor("out_x", shape, _mybir.dt.float32, kind="ExternalOutput").ap())
    xattn_moe_kernel(nc, *args)
    r = _run(nc, [arrays], core_ids=[0])
    return r.results[0]["out_x"]
```

```python
from contextlib import ExitStack

import concourse.bass as bass
from concourse import mybir

ALU = mybir.AluOpType
ACT = mybir.ActivationFunctionType
AX = mybir.AxisListType
F32 = mybir.dt.float32
F32R = mybir.dt.float32r

P = 128
BANK = 512
HEADS = 16
TOPK = 4
KEEP_GROUPS = 4
GROUPS = 8
EPS = 1e-5
BIG = 3.0e38


def xattn_moe_kernel(nc, x, ctx, mask, wo_w, wo_b, gw, gb, w1, b1, w3, b3, w2, b2,
                     sw1, sb1, sw3, sb3, sw2, sb2, out):
    B, S, D = x.shape
    SK = ctx.shape[1]
    SKE = SK + SK % 2
    KT = 3
    KP = SK // KT
    DH = D // HEADS
    DK = D // P
    E, _, INTER = w1.shape
    VC = 32
    NSH = sw1.shape[1] // INTER
    NE = E + NSH
    GE = E // GROUPS
    T = B * S
    NCH = 2
    CB = B // NCH
    CT = CB * S
    assert KP * KT == SK and INTER == P and DK == 2 and DH == 16 and NSH == 2 and CT <= BANK and B % 2 == 0

    NH = 2 * HEADS
    T_LAG, C_LAG, PV_LAG = 3, 3, 5
    RING = 8
    SR, TR = 2, 2
    PR = 4
    NKU = HEADS // 2
    NQU = 2
    NPREP = NKU + NQU
    PREP_AT = [0, 1, 2, 3, 5, 7, 9, 11, 12, 13]
    DRAIN_AT = PV_LAG - 1
    TAIL = (("turn", 2, "DVE"), ("ctxT", 4, "ACT"), ("proj", 6, "DVE"))

    def aux_plan(first, last):
        plan = []
        for half in range(2):
            if half == 0 or not last:
                for n, at in enumerate(PREP_AT):
                    plan.append((half * HEADS + at, "prep", n, half + 1, "DVE" if n % 2 else "ACT"))
        for ends in ([] if first else [0]) + [HEADS] + ([NH] if last else []):
            for kind, later, who in TAIL:
                plan.append((ends + DRAIN_AT + later, kind, 0, ends // HEADS - 1, who))
        plan.sort(key=lambda u: u[0])
        return plan

    NAUX = len(aux_plan(False, False))

    def aux_base(i):
        return NPREP if isinstance(i, int) and i == 0 else NPREP + NAUX * i - len(TAIL)

    def aux_bank(i, j):
        return (aux_base(0 if isinstance(i, int) and i == 0 else 1) + j) % 2

    def aux_reads(i, plan, m):
        full = [u[4] for u in aux_plan(False, False)]
        pair_d, pair_a = full.count("DVE"), full.count("ACT")
        assert pair_d + pair_a == NAUX and NAUX % 2 == 0 and full[-1] == "DVE"
        own = [u[4] for u in plan[:max(0, m)]]
        if isinstance(i, int) and i == 0:
            d, a = NPREP // 2, NPREP // 2
        else:
            late = [u[2] for u in TAIL]
            d, a = NPREP // 2 + pair_d * i - late.count("DVE"), NPREP // 2 + pair_a * i - late.count("ACT")
        return d + own.count("DVE") - (m < 0), a + own.count("ACT")

    def copied_by_dve(n):
        return n % 2 == 0

    def copies(n):
        d = sum(copied_by_dve(k) for k in range(n)) if n >= 0 else -sum(copied_by_dve(k) for k in range(n, 0))
        return d, n - d

    D_PAIR, A_PAIR = copies(NH)
    NSTEPS = NH + DRAIN_AT + TAIL[-1][1] + 1

    def wait(eng, s, value):
        if not isinstance(value, int) or value > 0:
            eng.wait_ge(s, value)

    scratch = nc.dram_tensor("gate_rows", (E, T), F32, kind="Internal").ap()

    with ExitStack() as st:
        def sb(name, shape, dt=F32):
            return st.enter_context(nc.sbuf_tensor(name, shape, dt))

        def sem(name):
            return st.enter_context(nc.semaphore(name))

        ps = st.enter_context(nc.psum_tensor("ps", [P, 8, BANK], F32))

        ident = sb("ident", [P, P])
        x_sb = sb("x_sb", [S, B, D])
        normed = sb("normed", [S, B, D])
        x2 = sb("x2", [S, B, D])
        wo_raw = sb("wo_raw", [P, DK, D])
        woT = sb("woT", [P, DK, D])
        wob = sb("wob", [S, D])
        gw_sb = sb("gw_sb", [P, DK, E])
        gb_sb = sb("gb_sb", [S, E])
        b1r = sb("b1r", [NE, P])
        b3r = sb("b3r", [NE, P])
        b1T = sb("b1T", [P, NE])
        b3T = sb("b3T", [P, NE])
        b2a = sb("b2a", [NE, D])
        stats = sb("stats", [S, B, 6])
        mv = sb("mv", [S, B, 2])
        veps = sb("veps", [S, B])
        std = sb("std", [S, B])
        rstd = sb("rstd", [S, B])
        wr = sb("wr", [P, 2, 3, D])
        x_in = sem("x_in")
        const_in = sem("const_in")
        ctx_in = [sem("ctx_in0"), sem("ctx_in1")]
        mask_in = [sem("mask_in0"), sem("mask_in1")]
        ident_zero = sem("ident_zero")
        ident_ok = sem("ident_ok")
        identr_ok = sem("identr_ok")
        b2_zero = sem("b2_zero")
        kT_zero = sem("kT_zero")
        kst_zero = [sem("kst_zero0"), sem("kst_zero1")]
        keys_hi = sem("keys_hi")
        queries_hi = sem("queries_hi")
        values_zero = sem("values_zero")
        ones_ok = sem("ones_ok")
        bias_T = sem("bias_T")
        bias_copied = sem("bias_copied")
        wo_copied = sem("wo_copied")
        dve_step = sem("dve_step")
        dve_step2 = sem("dve_step2")
        std_ok = sem("std_ok")
        var_ok = sem("var_ok")
        q_ok = sem("q_ok")
        pool_hi = sem("pool_hi")
        stacked = sem("stacked")
        values_ok = sem("values_ok")
        aux_full = sem("aux_full")
        aux_by_dve = sem("aux_by_dve")
        aux_by_act = sem("aux_by_act")
        scores = sem("scores")
        masked = sem("masked")
        exped = sem("exped")
        p_turned = sem("p_turned")
        pT_by_dve = sem("pT_by_dve")
        pT_by_act = sem("pT_by_act")
        pv_done = sem("pv_done")
        sums_ok = sem("sums_ok")
        rsum_ok = sem("rsum_ok")
        x2_ok = sem("x2_ok")
        stats_ok = sem("stats_ok")
        xn_ok = sem("xn_ok")
        std2_ok = sem("std2_ok")
        var2_ok = sem("var2_ok")

        def waits_apart(eng, *waits):
            values = [eng.to_reg(v) for _, v in waits]
            eng.wait_ge(ident_ok, 1)
            for (s, _), v in zip(waits, values):
                eng.wait_ge(s, v)

        PT_BANK = SR
        AUX = SR + TR
        SUM_BANK = AUX + 2
        assert SUM_BANK + 2 == 8

        def attention(block, sba):
            ctx_sb = sba("ctx_sb", [KP, 2, KT, D])
            mask_sb = sba("mask_sb", [S, 2, SK])
            KPE = KP + KP % 2
            kst = sba("kst", [KPE, 2, KT, HEADS, 4, DH], F32R)
            qst = sba("qst", [S, 2, HEADS, 4, DH], F32R)
            identr = sba("identr", [P, P], F32R)
            vaug = sba("vaug", [KP, 2, KT, HEADS, VC])
            kT = sba("kT", [P, 2, NKU, SKE], F32R)
            qT = sba("qT", [P, 2, HEADS // 2, S], F32R)
            nsm = sba("nsm", [S, RING, SK])
            nmax = sba("nmax", [S, RING])
            prob = sba("prob", [S, RING, SK])
            pT = sba("pT", [KP, PR, KT * S])
            sums = sba("sums", [P, HEADS // 4 * S])
            rsum = sba("rsum", [S, HEADS])
            att = sba("att", [S, D])
            attT = sba("attT", [P, DK, S])
            prj = sba("prj", [S, D])

            def keys_of(par):
                return ctx_sb[:, par].rearrange("p t (h c) -> p (t h) c", c=DH)

            def stack_of(par):
                return kst[0:KP, par].rearrange("p t h f c -> p (t h) f c")

            def one_of(t, b):
                return t[bass.ds(b, 1), :, :].rearrange("o a b -> (o a) b")

            @block.sync
            def _(sp):
                sp.dma_start(x_sb[:], x.rearrange("b s d -> s b d")).then_inc(x_in, 16)

                def load_context(b, par):
                    sp.dma_start(ctx_sb[:, par], one_of(ctx, b).rearrange("(t p) d -> p t d", p=KP)).then_inc(ctx_in[par], 16)

                def load_mask(b, par):
                    sp.dma_start(mask_sb[:, par], one_of(mask.rearrange("b o s k -> (b o) s k"), b)).then_inc(mask_in[par], 16)

                for b in range(2):
                    load_context(b, b)
                    load_mask(b, b)
                sp.dma_start(wo_raw[:], wo_w.rearrange("(t p) d -> p t d", p=P)).then_inc(const_in, 16)
                sp.dma_start(wob[:], wo_b.rearrange("(o d) -> o d", o=1).to_broadcast([S, D])).then_inc(const_in, 16)
                sp.dma_start(gw_sb[:], gw.rearrange("(t p) e -> p t e", p=P)).then_inc(const_in, 16)
                sp.dma_start(gb_sb[:], gb.rearrange("(o d) -> o d", o=1).to_broadcast([S, E])).then_inc(const_in, 16)
                sp.dma_start(b1r[0:NSH, :], sb1.rearrange("(t p) -> t p", p=P)).then_inc(const_in, 16)
                sp.dma_start(b1r[NSH:NE, :], b1).then_inc(const_in, 16)
                sp.dma_start(b3r[0:NSH, :], sb3.rearrange("(t p) -> t p", p=P)).then_inc(const_in, 16)
                sp.dma_start(b3r[NSH:NE, :], b3).then_inc(const_in, 16)
                sp.wait_ge(b2_zero, 1)
                sp.dma_start(b2a[0:E, :], b2).then_inc(const_in, 16)
                sp.dma_start(b2a[E:E + 1, :], sb2.rearrange("(o d) -> o d", o=1)).then_inc(const_in, 16)
                for slot in range(2):
                    cols = slice(slot * INTER, (slot + 1) * INTER)
                    load_expert(sp, slot, sw1[:, cols], sw3[:, cols], sw2[cols, :])
                with sp.Fori(1, B // 2) as i:
                    for par in range(2):
                        sp.wait_ge(stacked, 4 * (2 * i + par - 1))
                        sp.wait_ge(values_ok, 2 * i + par - 1)
                        load_context(2 * i + par, par)
                        sp.wait_ge(masked, NH * i - HEADS * (1 - par))
                        load_mask(2 * i + par, par)

            @block.gpsimd
            def _(pool):
                pool.memset(ident[:], 0.0).then_inc(ident_zero, 1)
                pool.wait_ge(ident_zero, 1)
                pool.affine_select(out=ident[:], in_=ident[:], compare_op=ALU.not_equal, fill=1.0, base=0,
                                   pattern=[[-1, P]], channel_multiplier=1).then_inc(ident_ok, 1)
                pool.memset(b2a[:], 0.0).then_inc(b2_zero, 1)
                pool.memset(kT[:, :, :, SK:SKE].bitcast(F32), 0.0).then_inc(kT_zero, 1)
                pool.wait_ge(ident_ok, 1)
                pool.tensor_copy(identr[:], ident[:]).then_inc(identr_ok, 1)
                pool.wait_ge(identr_ok, 1)
                pool.memset(kst[96:KPE, 1].bitcast(F32), 0.0).then_inc(kst_zero[1], 1)
                pool.wait_ge(kst_zero[1], 1)
                pool.memset(vaug[:], 0.0).then_inc(values_zero, 1)
                pool.wait_ge(values_zero, 1)
                pool.memset(vaug[:, :, :, :, DH:DH + 1].rearrange("p a t h c -> p (a t h) c"), 1.0).then_inc(ones_ok, 1)
                pool.wait_ge(ones_ok, 1)

                def queries(b, par):
                    qin = normed[:, bass.ds(b, 1), :].rearrange("s o (h c) -> s (o h) c", c=DH)
                    waits_apart(pool, (q_ok, b + 1))
                    for f in (0, 1):
                        pool.tensor_copy(qst[:, par, :, f, :], qin).then_inc(pool_hi, 1)
                    waits_apart(pool, (pool_hi, 4 * b - 2))
                    for f in (2, 3):
                        pool.tensor_tensor(qst[:, par, :, f, :], qin, qst[:, par, :, 0, :].bitcast(F32),
                                           ALU.subtract).then_inc(stacked, 1)

                def keys_lo(par):
                    for f in (1, 3):
                        pool.tensor_tensor(stack_of(par)[:, :, f, :], keys_of(par),
                                           stack_of(par)[:, :, 0, :].bitcast(F32), ALU.subtract).then_inc(stacked, 1)

                def values(par):
                    pool.tensor_copy(vaug[:, par, :, :, 0:DH],
                                     ctx_sb[:, par].rearrange("p t (h c) -> p t h c", c=DH)).then_inc(values_ok, 1)

                pool.wait_ge(keys_hi, 4)
                pool.wait_ge(stacked, 4)
                keys_lo(1)
                queries(1, 1)
                for par in range(2):
                    values(par)
                with pool.Fori(1, B // 2) as i:
                    for par in range(2):
                        b = 2 * i + par
                        waits_apart(pool, (ctx_in[par], 16 * i + 16), (scores, HEADS * (b - 2) + 1))
                        for f in (0, 2):
                            pool.tensor_copy(stack_of(par)[:, :, f, :], keys_of(par)).then_inc(pool_hi, 1)
                        queries(b, par)
                        keys_lo(par)
                        waits_apart(pool, (pv_done, HEADS * (b - 1)))
                        values(par)

            def prep_fill(pe, n, b, par, bank):
                auxr = ps[:, AUX + bank, :].bitcast(F32R)
                if n == 0:
                    pe.wait_ge(stacked, 4 * b + 4)
                if n < NQU:
                    for g in range(4):
                        h2 = n * 4 + g
                        last = nc.tensor.transpose(auxr[:, g * S:(g + 1) * S],
                                                   qst[:, par, 2 * h2:2 * h2 + 2].rearrange("s h f c -> s (h f c)"),
                                                   identr[0:S, 0:S])
                else:
                    g = n - NQU
                    for t in range(KT):
                        last = nc.tensor.transpose(auxr[:, t * KPE:(t + 1) * KPE],
                                                   kst[:, par, t, 2 * g:2 * g + 2].rearrange("s h f c -> s (h f c)"),
                                                   identr[0:KPE, 0:KPE])
                last.then_inc(aux_full, 1)

            def prep_read(n, par, bank):
                auxb = ps[:, AUX + bank, :]
                if n < NQU:
                    return (qT[:, par, 4 * n:4 * n + 4, :].rearrange("p g s -> p (g s)"), auxb[:, 0:4 * S])
                return (kT[:, par, n - NQU, 0:SK].rearrange("p (t k) -> p t k", t=KT),
                        auxb[:, 0:KT * KPE].rearrange("p (t k) -> p t k", t=KT)[:, :, 0:KP])

            @block.tensor
            def _(pe):
                pe.wait_ge(ident_ok, 1)
                pe.wait_ge(identr_ok, 1)
                for n in range(NPREP):
                    if n >= 2:
                        pe.wait_ge(aux_by_act if n % 2 == 0 else aux_by_dve, n // 2)
                    prep_fill(pe, n, 0, 0, n % 2)
                pe.wait_ge(const_in, 16 * 10)
                nc.tensor.transpose(ps[:, SUM_BANK, 0:NE], b1r[:], ident[0:NE, 0:NE])
                nc.tensor.transpose(ps[:, SUM_BANK, P:P + NE], b3r[:], ident[0:NE, 0:NE]).then_inc(bias_T, 1)
                for t in range(DK):
                    for k in range(DK):
                        ins = nc.tensor.transpose(ps[:, SUM_BANK + 1, (k * DK + t) * P:(k * DK + t + 1) * P],
                                                  wo_raw[:, t, k * P:(k + 1) * P], ident[:])
                ins.then_inc(bias_T, 1)

                def pair(i, first, last):
                    plan = aux_plan(first, last)

                    def unit(j):
                        _, kind, n, later, _ = plan[j]
                        bank = aux_bank(i, j)
                        auxb = ps[:, AUX + bank, :]
                        nd, na = aux_reads(i, plan, j if kind in ("ctxT", "proj") else j - 1)
                        pe.wait_ge(aux_by_dve, nd)
                        pe.wait_ge(aux_by_act, na)
                        if kind == "prep":
                            prep_fill(pe, n, 2 * i + later, later % 2, bank)
                            return
                        if kind == "turn":
                            pe.wait_ge(sums_ok, 2 * i + later + 1)
                            for g in range(HEADS // 4):
                                ins = nc.tensor.transpose(auxb[0:S, g * P:(g + 1) * P], sums[:, g * S:(g + 1) * S],
                                                          ident[:])
                        elif kind == "ctxT":
                            for k in range(DK):
                                ins = nc.tensor.transpose(auxb[:, k * S:(k + 1) * S], att[:, k * P:(k + 1) * P],
                                                          ident[0:S, 0:S])
                        else:
                            for k in range(DK):
                                ins = nc.tensor.matmul(auxb[0:S, 0:D], attT[:, k, :], woT[:, k, :],
                                                       start=(k == 0), stop=(k == DK - 1))
                        ins.then_inc(aux_full, 1)

                    j = 0
                    for n in range(NSTEPS if last else NH):
                        if n < NH:
                            half, h = n // HEADS, n % HEADS
                            r = 64 * (h % 2)
                            if h == 0:
                                done = [k for k, u in enumerate(plan) if u[1] == "prep" and u[3] == half]
                                nd, na = aux_reads(i, plan, done[-1] + 1 if done else 0)
                                pe.wait_ge(aux_by_dve, nd)
                                pe.wait_ge(aux_by_act, na)
                            wait(pe, masked, NH * i + n - SR + 1)
                            nc.tensor.matmul(ps[0:S, n % SR, 0:SKE], qT[r:r + 64, half, h // 2, :],
                                             kT[r:r + 64, half, h // 2, :], start=True, stop=True).then_inc(scores, 1)
                        d = n - T_LAG
                        if (d >= 0 or not first) and d < NH:
                            pe.wait_ge(exped, NH * i + d + 1)
                            nd, na = copies(d - TR + 1)
                            wait(pe, pT_by_dve, D_PAIR * i + nd)
                            wait(pe, pT_by_act, A_PAIR * i + na)
                            for t in range(KT):
                                ins = nc.tensor.transpose(ps[0:KP, PT_BANK + d % TR, t * S:(t + 1) * S],
                                                          prob[:, d % RING, t * KP:(t + 1) * KP], ident[0:S, 0:S])
                            ins.then_inc(p_turned, 1)
                        d = n - PV_LAG
                        if (d >= 0 or not first) and d < NH:
                            nd, na = copies(d + 1)
                            wait(pe, pT_by_dve, D_PAIR * i + nd)
                            wait(pe, pT_by_act, A_PAIR * i + na)
                            h = d % HEADS
                            if h == 0:
                                wait(pe, sums_ok, 2 * i + d // HEADS - 1)
                                pe.wait_ge(values_ok, 2 * i + d // HEADS + 1)
                                if first:
                                    pe.wait_ge(*((bias_copied, 2) if d == 0 else (wo_copied, 1)))
                            row = VC * (h % 4)
                            for t in range(KT):
                                ins = nc.tensor.matmul(ps[row:row + VC, SUM_BANK + (d // HEADS) % 2, h // 4 * S:(h // 4 + 1) * S],
                                                       vaug[:, (d // HEADS) % 2, t, h, :],
                                                       pT[:, d % PR, t * S:(t + 1) * S],
                                                       start=(t == 0), stop=(t == KT - 1))
                            ins.then_inc(pv_done, 1)
                        while j < len(plan) and plan[j][0] == n:
                            unit(j)
                            j += 1
                    assert j == len(plan)

                pair(0, True, False)
                with pe.Fori(1, B // 2 - 1) as i:
                    pair(i, False, False)
                pair(B // 2 - 1, False, True)

            @block.scalar
            def _(act):
                for par in range(2):
                    act.wait_ge(ctx_in[par], 16)
                    act.wait_ge(kst_zero[par], 1)
                    for f in (0, 2):
                        nc.scalar.copy(stack_of(par)[:, :, f, :], keys_of(par)).then_inc(keys_hi, 1)
                        if par == 0 and f == 0:
                            act.wait_ge(var_ok, 1)
                            nc.scalar.activation(std[:, 0:2], veps[:, 0:2], ACT.Sqrt).then_inc(std_ok, 1)

                def read_prep(n, par, bank):
                    dst, src = prep_read(n, par, bank)
                    nc.scalar.copy(dst, src).then_inc(aux_by_act, 1)

                act.wait_ge(kT_zero, 1)
                for n in range(NPREP):
                    if n % 2 == 0:
                        act.wait_ge(aux_full, n + 1)
                        read_prep(n, 0, n % 2)
                act.wait_ge(var_ok, 2)
                nc.scalar.activation(std[:, 2:B], veps[:, 2:B], ACT.Sqrt).then_inc(std_ok, 1)
                act.wait_ge(bias_T, 1)
                nc.scalar.copy(b1T[:], ps[:, SUM_BANK, 0:NE]).then_inc(bias_copied, 1)
                nc.scalar.copy(b3T[:], ps[:, SUM_BANK, P:P + NE]).then_inc(bias_copied, 1)

                def pair(i, first, last):
                    plan = aux_plan(first, last)
                    j = 0
                    for n in range(NSTEPS if last else NH):
                        d = n - C_LAG
                        if (d >= 0 or not first) and d < NH and not copied_by_dve(d):
                            act.wait_ge(p_turned, NH * i + d + 1)
                            wait(act, pv_done, NH * i + d - PR + 1)
                            nc.scalar.copy(pT[:, d % PR, :], ps[0:KP, PT_BANK + d % TR, 0:KT * S]).then_inc(pT_by_act, 1)
                        if n < NH:
                            act.wait_ge(masked, NH * i + n + 1)
                            wait(act, p_turned, NH * i + n - RING + 1)
                            nc.scalar.activation(prob[:, n % RING, :], nsm[:, n % RING, :], ACT.Exp, scale=-1.0,
                                                 bias=nmax[:, n % RING:n % RING + 1]).then_inc(exped, 1)
                        for ends in (0, HEADS, NH):
                            if n == ends + DRAIN_AT and not (first and ends == 0):
                                act.wait_ge(pv_done, NH * i + ends)
                                nc.scalar.copy(sums[:], ps[:, SUM_BANK + (ends // HEADS + 1) % 2, 0:HEADS // 4 * S]).then_inc(sums_ok, 1)
                        if n == NH + DRAIN_AT:
                            act.wait_ge(var2_ok, 1)
                            nc.scalar.activation(std[:, 0:B - 1], veps[:, 0:B - 1], ACT.Sqrt).then_inc(std2_ok, 1)
                        while j < len(plan) and plan[j][0] == n:
                            _, kind, k, later, who = plan[j]
                            if who == "ACT":
                                act.wait_ge(aux_full, aux_base(i) + j + 1)
                                if kind == "prep":
                                    read_prep(k, later % 2, aux_bank(i, j))
                                else:
                                    nc.scalar.copy(attT[:].rearrange("p k s -> p (k s)"),
                                                   ps[:, AUX + aux_bank(i, j), 0:DK * S]).then_inc(aux_by_act, 1)
                            j += 1

                pair(0, True, False)
                with act.Fori(1, B // 2 - 1) as i:
                    pair(i, False, False)
                pair(B // 2 - 1, False, True)

            @block.vector
            def _(dve):
                made = {"n": 0}

                def then_wait(ins):
                    made["n"] += 1
                    ins.then_inc(dve_step, 1)
                    dve.wait_ge(dve_step, made["n"])

                def statistics(b):
                    return nc.vector.bn_stats(stats[:, b, :], x_sb[:, b, :])

                def variances(lo, hi):
                    for b in range(lo, hi):
                        ins = nc.vector.bn_aggr(mv[:, b, :], stats[:, b, :])
                    then_wait(ins)
                    nc.vector.tensor_scalar(veps[:, lo:hi], mv[:, lo:hi, 1], EPS, None, ALU.add).then_inc(var_ok, 1)

                def normalise(b):
                    nc.vector.tensor_scalar(normed[:, b, :], x_sb[:, b, :], mv[:, b, 0:1], rstd[:, b:b + 1],
                                            ALU.subtract, ALU.mult).then_inc(q_ok, 1)

                def read_prep(n, par, bank):
                    dst, src = prep_read(n, par, bank)
                    nc.vector.tensor_copy(dst, src).then_inc(aux_by_dve, 1)

                nc.vector.memset(kst[96:KPE, 0].bitcast(F32), 0.0).then_inc(kst_zero[0], 1)
                dve.wait_ge(x_in, 16)
                statistics(0)
                then_wait(statistics(1))
                variances(0, 2)
                dve.wait_ge(std_ok, 1)
                then_wait(nc.vector.reciprocal(rstd[:, 0:2], std[:, 0:2]))
                normalise(0)
                normalise(1)
                qin = normed[:, 0, :].rearrange("s (h c) -> s h c", c=DH)
                dve.wait_ge(q_ok, 1)
                for f in (0, 1):
                    nc.vector.tensor_copy(qst[:, 0, :, f, :], qin).then_inc(queries_hi, 1)
                dve.wait_ge(queries_hi, 2)
                for f in (2, 3):
                    nc.vector.tensor_tensor(qst[:, 0, :, f, :], qin, qst[:, 0, :, 0, :].bitcast(F32),
                                            ALU.subtract).then_inc(stacked, 1)
                dve.wait_ge(keys_hi, 2)
                for f in (1, 3):
                    nc.vector.tensor_tensor(stack_of(0)[:, :, f, :], keys_of(0),
                                            stack_of(0)[:, :, 0, :].bitcast(F32), ALU.subtract).then_inc(stacked, 1)
                dve.wait_ge(kT_zero, 1)
                for b in range(2, B):
                    if b < B - 1:
                        statistics(b)
                    else:
                        then_wait(statistics(b))
                    if b % 2 == 1:
                        dve.wait_ge(aux_full, b - 1)
                        read_prep(b - 2, 0, (b - 2) % 2)
                variances(2, B)
                for n in range(B - 1, NPREP, 2):
                    dve.wait_ge(aux_full, n + 1)
                    read_prep(n, 0, n % 2)
                dve.wait_ge(std_ok, 2)
                then_wait(nc.vector.reciprocal(rstd[:, 2:B], std[:, 2:B]))

                def pair(i, first, last):
                    plan = aux_plan(first, last)
                    j = 0
                    for n in range(NSTEPS if last else NH):
                        d = n - C_LAG
                        if (d >= 0 or not first) and d < NH and copied_by_dve(d):
                            dve.wait_ge(p_turned, NH * i + d + 1)
                            wait(dve, pv_done, NH * i + d - PR + 1)
                            nc.vector.tensor_copy(pT[:, d % PR, :], ps[0:KP, PT_BANK + d % TR, 0:KT * S]
                                                  ).then_inc(pT_by_dve, 1)
                        if first and 1 <= n < B - 1:
                            normalise(n + 1)
                        if first and n == B:
                            dve.wait_ge(bias_T, 2)
                            nc.vector.tensor_copy(woT[:].rearrange("p k d -> p (k d)"),
                                                  ps[:, SUM_BANK + 1, :]).then_inc(wo_copied, 1)
                        if n < NH:
                            half = n // HEADS
                            if n % HEADS == 0:
                                dve.wait_ge(mask_in[half], 16 * i + 16)
                            two = [(scores, NH * i + n + 1), (exped, NH * i + n - RING + 1)]
                            if first:
                                for q, v in two:
                                    wait(dve, q, v)
                            else:
                                waits_apart(dve, *two)
                            nc.vector.tensor_tensor_reduce(
                                out=nsm[:, n % RING, :], in0=ps[0:S, n % SR, 0:SK], in1=mask_sb[:, half, :],
                                scale=-1.0, scalar=BIG, op0=ALU.add, op1=ALU.min,
                                accum_out=nmax[:, n % RING:n % RING + 1]).then_inc(masked, 1)
                        while j < len(plan) and plan[j][0] == n:
                            _, kind, k, later, who = plan[j]
                            b = 2 * i + later
                            auxb = ps[:, AUX + aux_bank(i, j), :]
                            if who == "DVE":
                                dve.wait_ge(aux_full, aux_base(i) + j + 1)
                            if kind == "prep" and who == "DVE":
                                read_prep(k, later % 2, aux_bank(i, j))
                            elif kind == "turn":
                                heads = auxb[0:S, :].rearrange("s (h c) -> s h c", c=VC)
                                nc.vector.reciprocal(rsum[:], heads[:, :, DH]).then_inc(rsum_ok, 1)
                                dve.wait_ge(rsum_ok, b + 1)
                                nc.vector.tensor_tensor(att[:].rearrange("s (h c) -> s h c", c=DH), heads[:, :, 0:DH],
                                                        rsum[:].unsqueeze(2).to_broadcast([S, HEADS, DH]),
                                                        ALU.mult).then_inc(aux_by_dve, 1)
                            elif kind == "proj":
                                xb = x_sb[:, bass.ds(b, 1), :].rearrange("s o d -> s (o d)")
                                x2b = x2[:, bass.ds(b, 1), :].rearrange("s o d -> s (o d)")
                                nc.vector.tensor_tensor(prj[:], auxb[0:S, 0:D], wob[:], ALU.add).then_inc(aux_by_dve, 1)
                                dve.wait_ge(aux_by_dve, aux_reads(i, plan, j + 1)[0])
                                nc.vector.scalar_tensor_tensor(x2b, prj[:], 0.0, xb, ALU.max, ALU.add).then_inc(x2_ok, 1)
                                dve.wait_ge(x2_ok, b + 1)
                                nc.vector.bn_stats(stats[:, bass.ds(b, 1), :].rearrange("s o d -> s (o d)"), x2b).then_inc(stats_ok, 1)
                            j += 1
                        if n == NH + C_LAG:
                            dve.wait_ge(stats_ok, B - 1)
                            for b in range(B - 1):
                                ins = nc.vector.bn_aggr(mv[:, b, :], stats[:, b, :])
                            then_wait(ins)
                            nc.vector.tensor_scalar(veps[:, 0:B - 1], mv[:, 0:B - 1, 1], EPS, None, ALU.add).then_inc(var2_ok, 1)
                        if n == NH + DRAIN_AT + TAIL[0][1]:
                            dve.wait_ge(std2_ok, 1)
                            then_wait(nc.vector.reciprocal(rstd[:, 0:B - 1], std[:, 0:B - 1]))
                            dve.wait_ge(stacked, 4 * B)
                            for b in range(B - 1):
                                nc.vector.tensor_scalar(normed[:, b, :], x2[:, b, :], mv[:, b, 0:1], rstd[:, b:b + 1],
                                                        ALU.subtract, ALU.mult).then_inc(xn_ok, 1)

                pair(0, True, False)
                with dve.Fori(1, B // 2 - 1) as i:
                    pair(i, False, False)
                pair(B // 2 - 1, False, True)

        w_in = [sem("w_in0"), sem("w_in1")]
        gate_in = [sem("gate_in0"), sem("gate_in1")]
        gate_out = sem("gate_out")
        xT_full = sem("xT_full")
        xf_by_act = sem("xf_by_act")
        xf_by_dve = sem("xf_by_dve")
        xhi_ok = sem("xhi_ok")
        xlo_ok = sem("xlo_ok")
        logits_ok = sem("logits_ok")
        lmax_ok = sem("lmax_ok")
        probs_ok = sem("probs_ok")
        cw_ok = sem("cw_ok")
        cw_turned = sem("cw_turned")
        cwT_ok = sem("cwT_ok")
        const_ok = sem("const_ok")
        whi_up = sem("whi_up")
        wlo_up = sem("wlo_up")
        whi_down = sem("whi_down")
        wlo_down = sem("wlo_down")
        h1_full = sem("h1_full")
        h3_full = sem("h3_full")
        silu_ok = sem("silu_ok")
        gated = sem("gated")
        h_ok = sem("h_ok")
        hhi_ok = sem("hhi_ok")
        hlo_ok = sem("hlo_ok")
        down_done = sem("down_done")
        y_by_act = sem("y_by_act")
        y_by_dve = sem("y_by_dve")
        y_turned = sem("y_turned")
        out_ok = sem("out_ok")
        out_sent = sem("out_sent")

        def load_expert(sp, slot, a1, a3, a2):
            sp.dma_start(wr[:, slot, 0:DK, 0:INTER], a1.rearrange("(k p) i -> p k i", p=P)).then_inc(w_in[slot], 16)
            sp.dma_start(wr[:, slot, 0:DK, INTER:D], a3.rearrange("(k p) i -> p k i", p=P)).then_inc(w_in[slot], 16)
            sp.dma_start(wr[:, slot, DK, :], a2).then_inc(w_in[slot], 16)

        def experts(block, sbe):
            xf = sbe("xf", [P, DK, T])
            xhi = sbe("xhi", [P, DK, T], F32R)
            xlo = sbe("xlo", [P, DK, T], F32R)
            whi = sbe("whi", [P, 2, 3, D], F32R)
            wlo = sbe("wlo", [P, 2, 3, D], F32R)
            lg = sbe("lg", [S, B, E])
            lmax = sbe("lmax", [S, B])
            ld = sbe("ld", [S, B, E])
            ex = sbe("ex", [S, B, E])
            esum = sbe("esum", [S, B])
            sc = sbe("sc", [S, B, E])
            pmax = sbe("pmax", [S, B * GROUPS, 2])
            pmin = sbe("pmin", [S, B * GROUPS, 2])
            top1 = sbe("top1", [S, B * GROUPS])
            lowm = sbe("lowm", [S, B * GROUPS])
            highm = sbe("highm", [S, B * GROUPS])
            top2 = sbe("top2", [S, B * GROUPS])
            gs = sbe("gs", [S, B, GROUPS])
            keep = sbe("keep", [S, B, GROUPS])
            keepm = sbe("keepm", [S, B, GROUPS])
            msc = sbe("msc", [S, B, E])
            sel = sbe("sel", [S, B, E])
            best = sbe("best", [S, B, 8])
            above = sbe("above", [S, B, E])
            equal = sbe("equal", [S, B, E])
            n_above = sbe("n_above", [S, B])
            prefix = sbe("prefix", [S, B, E])
            restart = sbe("restart", [S, B, E])
            restart_g = sbe("restart_g", [S, B, GROUPS])
            cw = sbe("cw", [S, B, NE])
            cwT = sbe("cwT", [NE, T])
            we = sbe("we", [P, 2, T])
            sil = sbe("sil", [P, 2, CT])
            tg = sbe("tg", [P, 2, CT])
            hf = sbe("hf", [P, 2, CT])
            hhi = sbe("hhi", [P, 2, CT], F32R)
            hlo = sbe("hlo", [P, 2, CT], F32R)
            yT = sbe("yT", [P, DK, T])
            o_sb = sbe("o_sb", [S, B, D])

            def up_ps(which, par):
                return ps[:, 2 * par + which, 0:CT]

            def y_ps(k, c):
                return ps[:, 4 + 2 * k + c, 0:CT]

            NU = 2 * NE
            NPAIR = NE // 2

            @block.sync
            def _(sp):
                def gate_row(e, slot):
                    sp.dma_start(we[:, slot, :], scratch[bass.ds(e, 1), :].to_broadcast([P, T])).then_inc(gate_in[slot], 16)

                def weights(place, slot):
                    for q in (whi_up, wlo_up, whi_down, wlo_down):
                        sp.wait_ge(q, place - 1)
                    e = place - NSH
                    load_expert(sp, slot, one(w1, e), one(w3, e), one(w2, e))

                def one(w, e):
                    return w[bass.ds(e, 1), :, :].rearrange("o a b -> (o a) b")

                for slot in range(2):
                    weights(NSH + slot, slot)
                for c in range(NCH):
                    sp.wait_ge(cwT_ok, c + 1)
                    sp.dma_start(scratch[:, c * CT:(c + 1) * CT], cwT[0:E, c * CT:(c + 1) * CT]).then_inc(gate_out, 16)
                sp.wait_ge(gate_out, 16 * NCH)
                gate_row(0, 0)
                gate_row(1, 1)
                with sp.Fori(2, NPAIR) as i:
                    for slot in range(2):
                        place = 2 * i + slot
                        weights(place, slot)
                        sp.wait_ge(gated, 2 * (place - 3))
                        gate_row(place - NSH, slot)

                for q in range(B // 2):
                    sp.wait_ge(out_ok, 2 * q + 2)
                    sp.dma_start(out[2 * q:2 * q + 2].rearrange("b s d -> s b d"),
                                 o_sb[:, 2 * q:2 * q + 2, :]).then_inc(out_sent, 16)
                sp.wait_ge(out_sent, 16 * (B // 2))

            @block.gpsimd
            def _(pool):
                pool.memset(restart[:], 1.0).then_inc(const_ok, 1)
                pool.memset(restart_g[:], 1.0).then_inc(const_ok, 1)
                pool.memset(cw[:], 1.0).then_inc(const_ok, 1)
                pool.wait_ge(const_ok, 3)
                pool.memset(restart[:, :, 0:1], 0.0).then_inc(const_ok, 1)
                pool.memset(restart_g[:, :, 0:1], 0.0).then_inc(const_ok, 1)

            @block.tensor
            def _(pe):
                for c in range(NCH):
                    pe.wait_ge(xn_ok, CB * (c + 1))
                    for k in range(DK):
                        for b in range(CB):
                            ins = nc.tensor.transpose(ps[:, 2 * c + k, b * S:(b + 1) * S],
                                                      normed[:, c * CB + b, k * P:(k + 1) * P], ident[0:S, 0:S])
                        ins.then_inc(xT_full, 1)
                for b in range(B):
                    if b % CB == 0:
                        pe.wait_ge(xf_by_act, b // CB + 1)
                        pe.wait_ge(xf_by_dve, b // CB + 1)
                    for k in range(DK):
                        ins = nc.tensor.matmul(ps[0:S, 4, b * E:(b + 1) * E], xf[:, k, b * S:(b + 1) * S],
                                               gw_sb[:, k, :], start=(k == 0), stop=(k == DK - 1))
                ins.then_inc(logits_ok, 1)

                pe.wait_ge(xhi_ok, 2 * NCH)
                pe.wait_ge(xlo_ok, 2 * NCH)

                def up(u, e, slot, c):
                    if c == 0:
                        pe.wait_ge(whi_up, e + 1)
                        pe.wait_ge(wlo_up, e + 1)
                    par = c
                    for which, full, read in ((0, h1_full, silu_ok), (1, h3_full, h_ok)):
                        if u is not None:
                            pe.wait_ge(read, u - 1)
                        n = 0
                        cols = slice(which * INTER, (which + 1) * INTER)
                        for k in range(DK):
                            toks = slice(c * CT, (c + 1) * CT)
                            for wt, xt in ((whi, xhi), (whi, xlo), (wlo, xhi)):
                                ins = nc.tensor.matmul(up_ps(which, par), wt[:, slot, k, cols], xt[:, k, toks],
                                                       start=(n == 0), stop=(n == 3 * DK - 1))
                                n += 1
                        ins.then_inc(full, 1)

                def down(u, e, slot, c, first=False, last=False):
                    if c == 0:
                        pe.wait_ge(whi_down, e + 1)
                        pe.wait_ge(wlo_down, e + 1)
                    pe.wait_ge(hhi_ok, u + 1)
                    order = [(whi, hhi, k) for k in range(DK)] + [(wlo, hhi, k) for k in range(DK)]
                    order += [(whi, hlo, k) for k in range(DK)]
                    for n, (wt, ht, k) in enumerate(order):
                        if n == 2 * DK:
                            pe.wait_ge(hlo_ok, u + 1)
                        ins = nc.tensor.matmul(y_ps(k, c), wt[:, slot, DK, k * P:(k + 1) * P], ht[:, c, :],
                                               start=first and n < DK, stop=last and n >= 2 * DK, skip_group_check=True)
                    ins.then_inc(down_done, 1)

                up(None, 0, 0, 0)
                up(None, 0, 0, 1)
                down(0, 0, 0, 0, first=True)
                up(2, 1, 1, 0)
                down(1, 0, 0, 1, first=True)
                up(3, 1, 1, 1)
                down(2, 1, 1, 0)
                pe.wait_ge(cw_ok, 1)
                pe.wait_ge(silu_ok, 3)
                pe.wait_ge(h_ok, 3)
                for c in range(NCH):
                    for b in range(CB):
                        ins = nc.tensor.transpose(ps[0:NE, c, b * S:(b + 1) * S], cw[:, c * CB + b, :],
                                                  ident[0:S, 0:S])
                    ins.then_inc(cw_turned, 1)
                for c in range(NCH):
                    pe.wait_ge(cwT_ok, c + 1)
                    for k in range(DK):
                        nc.tensor.matmul(y_ps(k, c), b2a[:, k * P:(k + 1) * P], cwT[:, c * CT:(c + 1) * CT],
                                         start=False, stop=False, skip_group_check=True)

                with pe.Fori(1, NPAIR) as i:
                    up(4 * i, 2 * i, 0, 0)
                    down(4 * i - 1, 2 * i - 1, 1, 1)
                    up(4 * i + 1, 2 * i, 0, 1)
                    down(4 * i, 2 * i, 0, 0)
                    up(4 * i + 2, 2 * i + 1, 1, 0)
                    down(4 * i + 1, 2 * i, 0, 1)
                    up(4 * i + 3, 2 * i + 1, 1, 1)
                    down(4 * i + 2, 2 * i + 1, 1, 0)
                down(NU - 1, NE - 1, 1, 1, last=True)

                for b in range(B):
                    c = b // CB
                    if b % CB == 0:
                        pe.wait_ge(y_by_act, c + 1)
                        pe.wait_ge(y_by_dve, c + 1)
                    for k in range(DK):
                        ins = nc.tensor.transpose(ps[0:S, b // 2, (b % 2) * D + k * P:(b % 2) * D + (k + 1) * P],
                                                  yT[:, k, b * S:(b + 1) * S], ident[:])
                    ins.then_inc(y_turned, 1)

            @block.scalar
            def _(act):
                act.wait_ge(var2_ok, 2)
                nc.scalar.activation(std[:, B - 1:B], veps[:, B - 1:B], ACT.Sqrt).then_inc(std2_ok, 1)
                for c in range(NCH):
                    act.wait_ge(xT_full, DK * c + 1)
                    nc.scalar.copy(xf[:, 0, c * CT:(c + 1) * CT], ps[:, DK * c, 0:CT]).then_inc(xf_by_act, 1)
                for n in range(2 * NCH):
                    c, k = n // DK, n % DK
                    act.wait_ge(xf_by_act if k == 0 else xf_by_dve, c + 1)
                    nc.scalar.copy(xhi[:, k, c * CT:(c + 1) * CT], xf[:, k, c * CT:(c + 1) * CT]).then_inc(xhi_ok, 1)

                def split_hi_up(e, slot, n):
                    act.wait_ge(w_in[slot], 48 * (n + 1))
                    if e is not None:
                        act.wait_ge(h3_full, 2 * e - 2)
                        act.wait_ge(wlo_up, e - 1)
                    nc.scalar.copy(whi[:, slot, 0:DK].rearrange("p k d -> p (k d)"),
                                   wr[:, slot, 0:DK].rearrange("p k d -> p (k d)")).then_inc(whi_up, 1)

                def split_hi_down(e, slot):
                    if e is not None:
                        act.wait_ge(down_done, 2 * e - 2)
                        act.wait_ge(wlo_down, e - 1)
                    nc.scalar.copy(whi[:, slot, DK], wr[:, slot, DK]).then_inc(whi_down, 1)

                for slot in range(2):
                    split_hi_up(None, slot, 0)
                    split_hi_down(None, slot)
                act.wait_ge(lmax_ok, 1)
                nc.scalar.activation(ex[:], ld[:], ACT.Exp).then_inc(probs_ok, 1)

                def silu(u, e, c):
                    waits_apart(act, (h1_full, u + 1))
                    nc.scalar.activation(sil[:, c, :], up_ps(0, c), ACT.Silu,
                                         bias=b1T[:, bass.ds(e, 1)]).then_inc(silu_ok, 1)

                def hi(u, c):
                    act.wait_ge(h_ok, u + 1)
                    nc.scalar.copy(hhi[:, c, :], hf[:, c, :]).then_inc(hhi_ok, 1)

                def pair(i, last, first=False):
                    for s in range(2):
                        e = 2 * i + s
                        for c in range(2):
                            u = 2 * e + c
                            silu(u, e, c)
                            if not (s == 0 and first) and not (last and s == 1):
                                if c == 0:
                                    split_hi_up(e + 1, 1 - s, i + s)
                                else:
                                    split_hi_down(e + 1, 1 - s)
                            hi(u, c)

                pair(0, False, True)
                with act.Fori(1, NPAIR - 1) as i:
                    pair(i, False)
                pair(NPAIR - 1, True)
                for n in range(2 * NCH):
                    c, k = n // DK, n % DK
                    if n % 2 == 0:
                        act.wait_ge(down_done, NU - 1 + c)
                        nc.scalar.copy(yT[:, k, c * CT:(c + 1) * CT], y_ps(k, c)).then_inc(y_by_act, 1)

            @block.vector
            def _(dve):
                steps = {"n": 0}

                def chained(ins):
                    steps["n"] += 1
                    ins.then_inc(gate_step, 1)
                    dve.wait_ge(gate_step, steps["n"])

                gate_step = dve_step2
                TT = nc.vector.tensor_tensor
                b = B - 1
                chained(nc.vector.bn_aggr(mv[:, b, :], stats[:, b, :]))
                nc.vector.tensor_scalar(veps[:, b:B], mv[:, b:B, 1], EPS, None, ALU.add).then_inc(var2_ok, 1)
                dve.wait_ge(std2_ok, 2)
                chained(nc.vector.reciprocal(rstd[:, b:B], std[:, b:B]))
                nc.vector.tensor_scalar(normed[:, b, :], x2[:, b, :], mv[:, b, 0:1], rstd[:, b:B],
                                        ALU.subtract, ALU.mult).then_inc(xn_ok, 1)
                for c in range(NCH):
                    dve.wait_ge(xT_full, DK * c + 2)
                    nc.vector.tensor_copy(xf[:, 1, c * CT:(c + 1) * CT], ps[:, DK * c + 1, 0:CT]).then_inc(xf_by_dve, 1)
                for n in range(2 * NCH):
                    c, k = n // DK, n % DK
                    toks = slice(c * CT, (c + 1) * CT)
                    dve.wait_ge(xf_by_act if k == 0 else xf_by_dve, c + 1)
                    dve.wait_ge(xhi_ok, n + 1)
                    TT(xlo[:, k, toks], xf[:, k, toks], xhi[:, k, toks].bitcast(F32), ALU.subtract).then_inc(xlo_ok, 1)

                def split_lo(e, slot, ks, hi_made, lo_made):
                    dve.wait_ge(hi_made, e + 1)
                    TT(wlo[:, slot, ks].rearrange("p k d -> p (k d)"), wr[:, slot, ks].rearrange("p k d -> p (k d)"),
                       whi[:, slot, ks].rearrange("p k d -> p (k d)").bitcast(F32), ALU.subtract).then_inc(lo_made, 1)

                def split_lo_up(e, slot):
                    split_lo(e, slot, slice(0, DK), whi_up, wlo_up)

                def split_lo_down(e, slot):
                    split_lo(e, slot, slice(DK, DK + 1), whi_down, wlo_down)

                def over(ap, shape):
                    return ap.unsqueeze(2).to_broadcast(shape)

                split_lo_up(0, 0)
                split_lo_down(0, 0)
                def unit_gate(u, slot, c, i):
                    dve.wait_ge(silu_ok, u + 1)
                    dve.wait_ge(gate_in[slot], 16 * i)
                    TT(tg[:, c, :], sil[:, c, :], we[:, slot, c * CT:(c + 1) * CT], ALU.mult).then_inc(gated, 1)

                def unit_h(u, e, c, shared=False):
                    dve.wait_ge(h3_full, u + 1)
                    if shared:
                        dve.wait_ge(silu_ok, u + 1)
                    else:
                        dve.wait_ge(gated, u + 1 - 2 * NSH)
                    nc.vector.scalar_tensor_tensor(hf[:, c, :], up_ps(1, c), b3T[:, bass.ds(e, 1)],
                                                   (sil if shared else tg)[:, c, :], ALU.add, ALU.mult).then_inc(h_ok, 1)

                def unit_lo(u, c):
                    dve.wait_ge(hhi_ok, u + 1)
                    TT(hlo[:, c, :], hf[:, c, :], hhi[:, c, :].bitcast(F32), ALU.subtract).then_inc(hlo_ok, 1)

                dve.wait_ge(logits_ok, 1)
                chained(TT(lg[:], ps[0:S, 4, 0:B * E].rearrange("s (b e) -> s b e", e=E),
                           gb_sb[:].unsqueeze(1).to_broadcast([S, B, E]), ALU.add))
                chained(nc.vector.tensor_reduce(lmax[:], lg[:], AX.X, ALU.max))
                TT(ld[:], lg[:], over(lmax[:], [S, B, E]), ALU.subtract).then_inc(lmax_ok, 1)
                split_lo_up(1, 1)
                dve.wait_ge(probs_ok, 1)
                chained(nc.vector.tensor_reduce(esum[:], ex[:], AX.X, ALU.add))
                chained(nc.vector.reciprocal(lmax[:], esum[:]))
                chained(TT(sc[:], ex[:], over(lmax[:], [S, B, E]), ALU.mult))
                unit_h(0, 0, 0, True)
                four = sc[:].rearrange("s b (g f) -> s (b g) f", f=GE)
                nc.vector.tensor_tensor(pmax[:], four[:, :, 0:2], four[:, :, 2:4], ALU.max)
                chained(TT(pmin[:], four[:, :, 0:2], four[:, :, 2:4], ALU.min))
                TT(top1[:], pmax[:, :, 0], pmax[:, :, 1], ALU.max)
                TT(lowm[:], pmax[:, :, 0], pmax[:, :, 1], ALU.min)
                chained(TT(highm[:], pmin[:, :, 0], pmin[:, :, 1], ALU.max))
                chained(TT(top2[:], lowm[:], highm[:], ALU.max))
                chained(TT(gs[:].rearrange("s b g -> s (b g)"), top1[:], top2[:], ALU.add))
                unit_lo(0, 0)
                split_lo_down(1, 1)

                def choose(chosen, values, width, count, starts):
                    for b in range(B):
                        ins = nc.vector.max(best[:, b, :], values[:, b, :])
                    chained(ins)
                    lim = best[:, :, count - 1:count].to_broadcast([S, B, width])
                    ab, eq, pf = above[:, :, 0:width], equal[:, :, 0:width], prefix
                    if width != E:
                        ab = above[:].rearrange("s b e -> s (b e)")[:, 0:B * width].rearrange("s (b w) -> s b w", w=width)
                        eq = equal[:].rearrange("s b e -> s (b e)")[:, 0:B * width].rearrange("s (b w) -> s b w", w=width)
                    pf = prefix[:].rearrange("s b e -> s (b e)")[:, 0:B * width]
                    TT(ab, values, lim, ALU.is_gt)
                    chained(TT(eq, values, lim, ALU.is_equal))
                    nc.vector.tensor_reduce(n_above[:], ab, AX.X, ALU.add)
                    chained(nc.vector.tensor_tensor_scan(pf, starts[:].rearrange("s b w -> s (b w)"),
                                                         eq.rearrange("s b w -> s (b w)"), 0.0, ALU.mult, ALU.add))
                    pf3 = pf.rearrange("s (b w) -> s b w", w=width)
                    chained(TT(pf3, pf3, over(n_above[:], [S, B, width]), ALU.add))
                    chained(nc.vector.scalar_tensor_tensor(eq, pf3, float(count), eq, ALU.is_le, ALU.mult))
                    chained(TT(chosen, ab, eq, ALU.add))

                dve.wait_ge(const_ok, 5)
                unit_h(1, 0, 1, True)
                choose(keep[:], gs[:], GROUPS, KEEP_GROUPS, restart_g)
                unit_lo(1, 1)
                chained(nc.vector.tensor_scalar(keepm[:], keep[:], -1.0, None, ALU.add))
                k4 = keep[:].rearrange("s b g -> s (b g)").unsqueeze(2).to_broadcast([S, B * GROUPS, GE])
                km4 = keepm[:].rearrange("s b g -> s (b g)").unsqueeze(2).to_broadcast([S, B * GROUPS, GE])
                m4 = msc[:].rearrange("s b (g f) -> s (b g) f", f=GE)
                chained(TT(m4, four, k4, ALU.mult))
                chained(TT(m4, m4, km4, ALU.add))
                unit_h(2, 1, 0, True)
                unit_lo(2, 0)
                choose(sel[:], msc[:], E, TOPK, restart)
                TT(cw[:, :, 0:E], sc[:], sel[:], ALU.mult).then_inc(cw_ok, 1)
                unit_h(3, 1, 1, True)
                split_lo_up(2, 0)
                for c in range(NCH):
                    dve.wait_ge(cw_turned, c + 1)
                    nc.vector.tensor_copy(cwT[:, c * CT:(c + 1) * CT], ps[0:NE, c, 0:CT]).then_inc(cwT_ok, 1)
                split_lo_down(2, 0)
                unit_lo(3, 1)

                def pair(i, last):
                    for s in range(2):
                        e = 2 * i + s
                        for c in range(2):
                            u = 2 * e + c
                            unit_gate(u, s, c, i)
                            unit_h(u, e, c)
                            if not (last and s == 1):
                                if c == 0:
                                    split_lo_up(e + 1, 1 - s)
                                else:
                                    split_lo_down(e + 1, 1 - s)
                            unit_lo(u, c)

                with dve.Fori(1, NPAIR - 1) as i:
                    pair(i, False)
                pair(NPAIR - 1, True)
                for n in range(2 * NCH):
                    c, k = n // DK, n % DK
                    if n % 2 == 1:
                        dve.wait_ge(down_done, NU - 1 + c)
                        nc.vector.tensor_copy(yT[:, k, c * CT:(c + 1) * CT], y_ps(k, c)).then_inc(y_by_dve, 1)
                for b in range(B):
                    dve.wait_ge(y_turned, 2 * (b // 2) + 2)
                    TT(o_sb[:, b, :], ps[0:S, b // 2, (b % 2) * D:(b % 2 + 1) * D], x2[:, b, :], ALU.add).then_inc(out_ok, 1)

        with ExitStack() as own:
            attention(own.enter_context(nc.Block()), lambda n, s, d=F32: own.enter_context(nc.sbuf_tensor(n, s, d)))
        with ExitStack() as own:
            experts(own.enter_context(nc.Block()), lambda n, s, d=F32: own.enter_context(nc.sbuf_tensor(n, s, d)))


_INS = ["x", "ctx_1024", "mask_Bx1xSxS2_ff0", "L0_xattn_wo_w", "L0_xattn_wo_b", "L0_ffn_gw", "L0_ffn_gb",
        "L0_ffn_w1", "L0_ffn_b1", "L0_ffn_w3", "L0_ffn_b3", "L0_ffn_w2", "L0_ffn_b2", "L0_ffn_sw1",
        "L0_ffn_sb1", "L0_ffn_sw3", "L0_ffn_sb3", "L0_ffn_sw2", "L0_ffn_sb2"]


def kernel(**inputs):
    import numpy as _np
    import concourse.bacc as _bacc
    from concourse import mybir as _mybir
    from concourse.bass_utils import run_bass_kernel_spmd as _run

    nc = _bacc.Bacc("TRN2", target_bir_lowering=False, num_devices=1)
    arrays, args = {}, []
    for name in _INS:
        a = _np.ascontiguousarray(inputs[name])
        arrays[f"in_{name}"] = a
        args.append(nc.dram_tensor(f"in_{name}", a.shape, _mybir.dt.from_np(a.dtype), kind="ExternalInput").ap())
    shape = inputs["x"].shape
    args.append(nc.dram_tensor("out_x", shape, _mybir.dt.float32, kind="ExternalOutput").ap())
    xattn_moe_kernel(nc, *args)
    r = _run(nc, [arrays], core_ids=[0])
    return r.results[0]["out_x"]
```
